# Optimizing a Trainium2 kernel written in Bass

```python
import numpy as np
import jax
import jax.numpy as jnp

def _softmax(x, axis=-1):
    return jax.nn.softmax(x, axis=axis)

def _gelu(x):
    return jax.nn.gelu(x, approximate=True)

def _silu(x):
    return jax.nn.silu(x)

def _sigmoid(x):
    return jax.nn.sigmoid(x)

def _layernorm(x, axis=-1, eps=1e-05):
    m = jnp.mean(x, axis=axis, keepdims=True)
    v = jnp.var(x, axis=axis, keepdims=True)
    return (x - m) / jnp.sqrt(v + eps)

def _scatter_add(tgt, idx, src, axis=0):
    return tgt.at[idx].add(src)

def _segment_sum(src, seg, n):
    return jax.ops.segment_sum(src, seg, n)
kernel_name = 'mk_decoder_postln_d1_seqx_r8_d7e14a'

def setup_inputs(seed: int=0):
    np.random.seed(seed)
    _w = jnp.asarray

    def _rec_inputs():
        import jax
        import jax.numpy as jnp
        _rk = jax.random.key(seed)
        x = 7.22e-05 + 1 * jax.random.normal(jax.random.fold_in(_rk, 1), (2, 512, 128), jnp.float32)
        _lenS = 512 - jax.random.randint(jax.random.fold_in(_rk, 7), (2,), 0, max(1, 512 // 4) + 1, jnp.int32)
        _lenS2 = 154 - jax.random.randint(jax.random.fold_in(_rk, 8), (2,), 0, max(1, 154 // 4) + 1, jnp.int32)
        _ctx_1024P = jax.random.normal(jax.random.fold_in(_rk, 11), (2, 16, 128), jnp.float32)
        _ctx_1024c = jax.random.dirichlet(jax.random.fold_in(_rk, 511), 0.3 * jnp.ones((16,), jnp.float32), (2, 154))
        _ctx_1024t = jnp.einsum('bsk,bkd->bsd', _ctx_1024c, _ctx_1024P)
        _ctx_1024t = _ctx_1024t * jax.lax.rsqrt(jnp.mean(jnp.square(_ctx_1024t)) + 1e-12) * 0.953939
        ctx_1024 = -1.39393e-06 + 0.999914 * (_ctx_1024t + 0.3 * jax.random.normal(jax.random.fold_in(_rk, 611), (2, 154, 128), jnp.float32))
        return (x, ctx_1024)
    x, ctx_1024 = _rec_inputs()

    def _L0_attn_setup():
        import jax, jax.numpy as jnp
        import numpy as np
        B, M, D, H = (2, 256, 128, 16)

        def _rope(x):
            b, m, d = x.shape
            i = jnp.arange(d // 2, dtype=jnp.float32)
            theta = 10000.0 ** (-2.0 * (i - 1.0) / d)
            ang = jnp.arange(m, dtype=jnp.float32)[:, None] * theta[None, :]
            c, s = (jnp.cos(ang), jnp.sin(ang))
            xe, xo = (x[..., 0::2], x[..., 1::2])
            ye = xe * c + xo * s
            yo = -xe * s + xo * c
            return jnp.stack([ye, yo], axis=-1).reshape(b, m, d)
        key = jax.random.key(seed)
        ks = jax.random.split(key, 8)
        w = lambda k, shape: jax.random.normal(k, shape, jnp.float32) * 0.02
        return {'x': jax.random.normal(ks[0], (B, M, D), jnp.float32), 'wq': w(ks[1], (D, D)), 'wk': w(ks[2], (D, D)), 'wv': w(ks[3], (D, D)), 'in_proj_w': w(ks[4], (3 * D, D)), 'in_proj_b': w(ks[5], (3 * D,)), 'out_w': w(ks[6], (D, D)), 'out_b': w(ks[7], (D,))}
    _L0_attn_all = _L0_attn_setup()
    _L0_attn_in = {k: v for k, v in _L0_attn_all.items() if k in ('wq', 'wk', 'wv', 'in_proj_w', 'in_proj_b', 'out_w', 'out_b')}
    del _L0_attn_all

    def _L0_xattn_setup():
        import jax, jax.numpy as jnp
        import numpy as np
        DIM = 128
        N_HEADS = 16
        HEAD_DIM = DIM // N_HEADS
        GAMMA = 10.0

        def larope_cos_sin(seq_len, gamma, head_dim):
            inv_freq = 1.0 / 10000.0 ** (jnp.arange(0, head_dim, 2, dtype=jnp.float32) / head_dim)
            t = jnp.arange(seq_len, dtype=jnp.float32)
            freqs = jnp.outer(gamma * (t / seq_len), inv_freq)
            emb = jnp.concatenate([freqs, freqs], axis=-1)
            return (jnp.cos(emb), jnp.sin(emb))

        def apply_rope(x, cos, sin):
            d = x.shape[-1] // 2
            x1, x2 = (x[..., :d], x[..., d:])
            c = cos[None, None, :, :d]
            s = sin[None, None, :, :d]
            return jnp.concatenate([x1 * c - x2 * s, x1 * s + x2 * c], axis=-1)
        key = jax.random.key(seed)
        ks = jax.random.split(key, 11)
        B, Lq, Lk = (4, 256, 128)
        std = 1.0 / np.sqrt(DIM)
        inp = {'query': jax.random.normal(ks[0], (B, Lq, DIM), dtype=jnp.float32), 'key': jax.random.normal(ks[1], (B, Lk, DIM), dtype=jnp.float32), 'value': jax.random.normal(ks[2], (B, Lk, DIM), dtype=jnp.float32), 'Wq': jax.random.normal(ks[3], (DIM, DIM), dtype=jnp.float32) * std, 'bq': jnp.zeros((DIM,), dtype=jnp.float32), 'Wk': jax.random.normal(ks[4], (DIM, DIM), dtype=jnp.float32) * std, 'bk': jnp.zeros((DIM,), dtype=jnp.float32), 'Wv': jax.random.normal(ks[5], (DIM, DIM), dtype=jnp.float32) * std, 'bv': jnp.zeros((DIM,), dtype=jnp.float32), 'Wo': jax.random.normal(ks[6], (DIM, DIM), dtype=jnp.float32) * std, 'bo': jnp.zeros((DIM,), dtype=jnp.float32)}
        return inp
    _L0_xattn_all = _L0_xattn_setup()
    _L0_xattn_in = {k: v for k, v in _L0_xattn_all.items() if k in ('Wq', 'bq', 'Wk', 'bk', 'Wv', 'bv', 'Wo', 'bo')}
    del _L0_xattn_all

    def _L0_ffn_setup():
        import jax, jax.numpy as jnp
        import numpy as np
        TOP_K = 2
        key = jax.random.key(seed)
        k0, k1, k2, k3, k4 = jax.random.split(key, 5)
        B, S, H, I, E = (1, 512, 128, 256, 8)
        hidden_states = jax.random.normal(k0, (B, S, H), dtype=jnp.float32)
        wg = jax.random.normal(k1, (E, H), dtype=jnp.float32) * 0.02
        w1 = jax.random.normal(k2, (E, I, H), dtype=jnp.float32) * 0.02
        w3 = jax.random.normal(k3, (E, I, H), dtype=jnp.float32) * 0.02
        w2 = jax.random.normal(k4, (E, H, I), dtype=jnp.float32) * 0.02
        return {'hidden_states': hidden_states, 'wg': wg, 'w1': w1, 'w3': w3, 'w2': w2}
    _L0_ffn_all = _L0_ffn_setup()
    _L0_ffn_in = {k: v for k, v in _L0_ffn_all.items() if k in ('wg', 'w1', 'w3', 'w2')}
    del _L0_ffn_all
    return {'x': x, 'ctx_1024': ctx_1024, 'L0_attn_wq': _L0_attn_in['wq'], 'L0_attn_wk': _L0_attn_in['wk'], 'L0_attn_wv': _L0_attn_in['wv'], 'L0_attn_in_proj_w': _L0_attn_in['in_proj_w'], 'L0_attn_in_proj_b': _L0_attn_in['in_proj_b'], 'L0_attn_out_w': _L0_attn_in['out_w'], 'L0_attn_out_b': _L0_attn_in['out_b'], 'L0_xattn_Wq': _L0_xattn_in['Wq'], 'L0_xattn_bq': _L0_xattn_in['bq'], 'L0_xattn_Wk': _L0_xattn_in['Wk'], 'L0_xattn_bk': _L0_xattn_in['bk'], 'L0_xattn_Wv': _L0_xattn_in['Wv'], 'L0_xattn_bv': _L0_xattn_in['bv'], 'L0_xattn_Wo': _L0_xattn_in['Wo'], 'L0_xattn_bo': _L0_xattn_in['bo'], 'L0_ffn_wg': _L0_ffn_in['wg'], 'L0_ffn_w1': _L0_ffn_in['w1'], 'L0_ffn_w3': _L0_ffn_in['w3'], 'L0_ffn_w2': _L0_ffn_in['w2']}

def reference(x, ctx_1024, L0_attn_wq, L0_attn_wk, L0_attn_wv, L0_attn_in_proj_w, L0_attn_in_proj_b, L0_attn_out_w, L0_attn_out_b, L0_xattn_Wq, L0_xattn_bq, L0_xattn_Wk, L0_xattn_bk, L0_xattn_Wv, L0_xattn_bv, L0_xattn_Wo, L0_xattn_bo, L0_ffn_wg, L0_ffn_w1, L0_ffn_w3, L0_ffn_w2):
    import jax
    import jax.numpy as jnp

    def _L0_attn_ref(x, wq, wk, wv, in_proj_w, in_proj_b, out_w, out_b):
        import jax, jax.numpy as jnp
        import numpy as np
        B, M, D, H = (2, 256, 128, 16)

        def _rope(x):
            b, m, d = x.shape
            i = jnp.arange(d // 2, dtype=jnp.float32)
            theta = 10000.0 ** (-2.0 * (i - 1.0) / d)
            ang = jnp.arange(m, dtype=jnp.float32)[:, None] * theta[None, :]
            c, s = (jnp.cos(ang), jnp.sin(ang))
            xe, xo = (x[..., 0::2], x[..., 1::2])
            ye = xe * c + xo * s
            yo = -xe * s + xo * c
            return jnp.stack([ye, yo], axis=-1).reshape(b, m, d)
        b, m, d = x.shape
        h = H
        hd = d // h
        q = _rope(x @ wq.T)
        k = _rope(x @ wk.T)
        v = _rope(x @ wv.T)
        wqi, wki, wvi = jnp.split(in_proj_w, 3, axis=0)
        bqi, bki, bvi = jnp.split(in_proj_b, 3, axis=0)
        qh = (q @ wqi.T + bqi).reshape(b, m, h, hd)
        kh = (k @ wki.T + bki).reshape(b, m, h, hd)
        vh = (v @ wvi.T + bvi).reshape(b, m, h, hd)
        scores = jnp.einsum('bqhd,bkhd->bhqk', qh, kh) / jnp.sqrt(jnp.float32(hd))
        causal = jnp.tril(jnp.ones((m, m), dtype=bool))
        scores = jnp.where(causal, scores, jnp.float32(-jnp.inf))
        attn = jax.nn.softmax(scores, axis=-1)
        o = jnp.einsum('bhqk,bkhd->bqhd', attn, vh).reshape(b, m, d)
        return o @ out_w.T + out_b

    def _L0_xattn_ref(query, key, value, Wq, bq, Wk, bk, Wv, bv, Wo, bo):
        import jax, jax.numpy as jnp
        import numpy as np
        DIM = 128
        N_HEADS = 16
        HEAD_DIM = DIM // N_HEADS
        GAMMA = 10.0

        def larope_cos_sin(seq_len, gamma, head_dim):
            inv_freq = 1.0 / 10000.0 ** (jnp.arange(0, head_dim, 2, dtype=jnp.float32) / head_dim)
            t = jnp.arange(seq_len, dtype=jnp.float32)
            freqs = jnp.outer(gamma * (t / seq_len), inv_freq)
            emb = jnp.concatenate([freqs, freqs], axis=-1)
            return (jnp.cos(emb), jnp.sin(emb))

        def apply_rope(x, cos, sin):
            d = x.shape[-1] // 2
            x1, x2 = (x[..., :d], x[..., d:])
            c = cos[None, None, :, :d]
            s = sin[None, None, :, :d]
            return jnp.concatenate([x1 * c - x2 * s, x1 * s + x2 * c], axis=-1)
        B, Lq, _ = query.shape
        Lk = key.shape[1]
        scale = HEAD_DIM ** (-0.5)

        def proj(x, W, b, L):
            y = x @ W.T + b
            return y.reshape(B, L, N_HEADS, HEAD_DIM).transpose(0, 2, 1, 3)
        q = proj(query, Wq, bq, Lq)
        k = proj(key, Wk, bk, Lk)
        v = proj(value, Wv, bv, Lk)
        q_cos, q_sin = larope_cos_sin(Lq, GAMMA, HEAD_DIM)
        k_cos, k_sin = larope_cos_sin(Lk, GAMMA, HEAD_DIM)
        q = apply_rope(q, q_cos, q_sin)
        k = apply_rope(k, k_cos, k_sin)
        scores = jnp.einsum('bhqd,bhkd->bhqk', q, k) * scale
        attn = jax.nn.softmax(scores, axis=-1)
        out = jnp.einsum('bhqk,bhkd->bhqd', attn, v)
        out = out.transpose(0, 2, 1, 3).reshape(B, Lq, DIM)
        return out @ Wo.T + bo

    def _L0_ffn_ref(hidden_states, wg, w1, w3, w2):
        import jax, jax.numpy as jnp
        import numpy as np
        TOP_K = 2
        orig_shape = hidden_states.shape
        H = orig_shape[-1]
        E = wg.shape[0]
        x = hidden_states.reshape(-1, H)
        router_logits = x @ wg.T
        probs = jax.nn.softmax(router_logits, axis=-1)
        topk_w, topk_idx = jax.lax.top_k(probs, TOP_K)
        topk_w = topk_w / jnp.sum(topk_w, axis=-1, keepdims=True)
        expert_w = jnp.sum(jax.nn.one_hot(topk_idx, E, dtype=x.dtype) * topk_w[..., None], axis=1)
        h1 = jnp.einsum('th,eih->tei', x, w1)
        h3 = jnp.einsum('th,eih->tei', x, w3)
        y = jnp.einsum('tei,ehi->teh', jax.nn.silu(h1) * h3, w2)
        out = jnp.einsum('te,teh->th', expert_w, y)
        return out.reshape(orig_shape)
    x = _layernorm(x + _L0_attn_ref(x, L0_attn_wq, L0_attn_wk, L0_attn_wv, L0_attn_in_proj_w, L0_attn_in_proj_b, L0_attn_out_w, L0_attn_out_b), axis=-1)
    x = _layernorm(x + _L0_xattn_ref(x, ctx_1024, ctx_1024, L0_xattn_Wq, L0_xattn_bq, L0_xattn_Wk, L0_xattn_bk, L0_xattn_Wv, L0_xattn_bv, L0_xattn_Wo, L0_xattn_bo), axis=-1)
    x = _layernorm(x + _L0_ffn_ref(x, L0_ffn_wg, L0_ffn_w1, L0_ffn_w3, L0_ffn_w2), axis=-1)
    return x

_drawn_inputs = setup_inputs


def setup_inputs(seed=0):
    import zlib

    import numpy as np

    out = dict(_drawn_inputs(seed))
    spreads = {'L0_xattn_bq': (0.0, 0.378),
     'L0_xattn_bk': (0.0, 0.8),
     'L0_xattn_bv': (0.0, 0.1),
     'L0_xattn_bo': (0.0, 0.1)}
    factors = {'L0_attn_wq': 8.0,
     'L0_attn_wk': 8.0,
     'L0_attn_wv': 8.0,
     'L0_attn_in_proj_w': 8.0,
     'L0_attn_in_proj_b': 8.0,
     'L0_attn_out_w': 8.0,
     'L0_attn_out_b': 2.995,
     'L0_ffn_wg': 8.0,
     'L0_ffn_w1': 8.0,
     'L0_ffn_w3': 8.0,
     'L0_ffn_w2': 8.0}
    for name, (base, spread) in spreads.items():
        noise = np.random.default_rng([zlib.crc32(name.encode()), seed]).standard_normal(out[name].shape)
        drawn = base * np.exp(spread * noise) if base else spread * noise
        out[name] = jnp.asarray(drawn.astype(out[name].dtype))
    for name, factor in factors.items():
        out[name] = (out[name] * factor).astype(out[name].dtype)
    return out
```

```python
import numpy as np

import concourse.bass as bass
from concourse import mybir
from contextlib import ExitStack

FP32 = mybir.dt.float32
BF16 = mybir.dt.bfloat16
U32 = mybir.dt.uint32
ALU = mybir.AluOpType
ACT = mybir.ActivationFunctionType
AX = mybir.AxisListType

B, S, D = 2, 512, 128
SC = 154
H, HD = 16, 8
G = 4
NG = H // G
QT = S // 128
E, I = 8, 256
FT = E * I // 128
PARTS = 3
ROWS = PARTS * PARTS * HD
KR = 96
SCP = 160
TAIL = SC - 128
NEG = -1e30
SCALE = float(np.float32(HD) ** np.float32(-0.5))
EPS = 1e-5
NU = 2 * B * NG

W_A = {n: i for i, n in enumerate(["wq", "wk", "wv", "iq", "iqs", "ik", "iks", "iv", "ivs", "out"])}
W_X = {n: i for i, n in enumerate(["q", "qs", "k", "ks", "v", "o"])}
C_CA, C_SA, C_CQ, C_SQ = 0, S, 2 * S, 3 * S
C_CK, C_SK = 4 * S, 4 * S + SC
C_ID = 4 * S + 2 * SC
C_IOTA = C_ID + 128
C_POW = C_IOTA + E
NC32 = C_POW + QT
H_ID, H_MA, H_MB, H_SEL = 0, 128, 256, 384
NC16 = H_SEL + E * 128


def unit(u):
    return u // (B * NG), u // NG % B, u % NG


def a_banks(u):
    if unit(u)[0] == 0:
        out = []
        for i in range(QT):
            n = min(G, QT // (i + 1)) if i < 2 else 1
            for j in range(0, G, n):
                out.append(([(i, j + k) for k in range(n)], 128 * (i + 1)))
        return out
    blocks = [(i, j) for i in range(QT) for j in range(G)]
    return [(blocks[k:k + 3], SC) for k in range(0, QT * G, 3)]


def b_banks(u):
    if unit(u)[0] == 0:
        out = [[(0, j, 0)] for j in range(G)]
        out += [[(1, j, 0), (3, j, S - 128)] for j in range(G)]
        out += [[(2, j, 0), (2, j + 1, 256)] for j in range(0, G, 2)]
        return out
    return [[(0, j, 0)] for j in range(G)] + [[(1, None, 0)]]


def a_base(u):
    return sum(len(a_banks(v)) for v in range(u))


def b_base(u):
    return sum(len(b_banks(v)) for v in range(u))


def make_plan():
    items = []
    n = [0]

    def at(t, kind, *args):
        items.append((t, n[0], kind, args))
        n[0] += 1

    t = -60.0
    for b in range(B):
        for w in ("q", "k"):
            at(t, "U", b, w)
            at(t + 1, "H", b, w)
            t += 0.5
        t += 2
        at(t, "SPLIT", b, "q"); at(t + 0.1, "SPLIT", b, "k")
        at(t + 0.2, "STACK", 0, b)
        at(t + 0.3, "U", b, "v")
        at(t + 0.4, "VH", b)
        t += 2
    at(t, "CK")
    at(t + 0.1, "STACKCK")
    at(t + 0.2, "CV")
    start, bt_end, stacked = 0.0, 0.0, {}
    for u in range(NU):
        st, b, g = unit(u)
        na = len(a_banks(u))
        nb = len(b_banks(u))
        if st == 1 and g == 0:
            start = max(start, stacked[b] + STACK_LAG)
        width = max(na, nb)
        for k in range(na):
            at(start + k, "A", u, k)
        at(start + na + MT_LAG, "MT", u)
        bt = max(start + na + B_LAG, bt_end)
        bt_end = bt + width
        step = width / nb
        for k in range(nb):
            at(bt + (k + 1) * step - 0.7, "B", u, k)
        if st == 0:
            at(bt + 5 * step + PV_LAG, "PV", u, 0)
            at(bt + 9 * step + PV_LAG, "PV", u, 1)
            at(bt + 9.1 * step + PV_LAG, "PV", u, 3)
            at(bt + 10.5 * step + PV_LAG, "PV", u, 2)
        else:
            at(bt + 4.5 * step + PV_LAG, "PV", u, 0)
            at(bt + 5.5 * step + PV_LAG, "PV", u, 1)
        at(bt + width + PV_LAG + 1.5, "POC", u)
        at(bt + width + PV_LAG + 3, "OT", u)
        if g == NG - 1:
            t = bt + width + PV_LAG + 4.5
            at(t, "ONT", st, b)
            at(t + 0.7, "OP", st, b)
            at(t + 0.9, "LN", st, b)
            at(t + 3.5, "XT", st, b)
            if st == 0:
                at(t + 4.5, "CQ", b)
                at(t + 4.6, "STACK", 1, b)
                stacked[b] = t + 4.6
            else:
                at(t + 4.5, "LG", b)
                at(t + 5.2, "GATE", b)
                at(t + 7.5, "WT", b)
        if u == NU - 1:
            end = bt + width + PV_LAG + 2
        start += width
    for b in range(B):
        for e in range(E):
            at(end + FT * b + 2 * e - 1.6, "BC", b, e)
        for f in range(FT):
            at(end + FT * b + f, "F1", b, f)
            at(end + FT * b + f + 2.6, "F2", b, f)
        t = end + FT * (b + 1) + 2
        at(t, "YE", b)
        at(t + 0.1, "YT", b)
        at(t + 0.2, "LN", 2, b)
        at(t + 0.3, "OUT", b)
    items.sort(key=lambda x: (x[0], x[1]))
    return [(kind, args) for _, _, kind, args in items]


MT_LAG, B_LAG, PV_LAG, STACK_LAG = 1.5, 8.0, 1.0, 6.0
PLAN = make_plan()

JOBS = {"U": 1, "H": 1, "VH": 1, "CK": 2, "CV": 1, "MT": 1, "OT": 1, "ONT": 1, "OP": 1, "XT": 1,
        "CQ": 2, "LG": 1, "WT": 1, "BC": 1, "YT": 1}


def job_numbers():
    numbers, n = {}, 0
    for item in PLAN:
        if item[0] in JOBS:
            numbers[item] = n
            n += JOBS[item[0]]
    return numbers


JOB = job_numbers()


def layer_kernel(nc, xt_d, x_d, ctxt_d, wa_d, wx_d, wg_d, bcol_d, brow_d, c32_d, c16_d, tail_d, w1_d, w3_d, w2_d, out_d):
    scr_q = nc.dram_tensor("scr_q", [2 * B, NG, PARTS, 32, S], BF16, kind="Internal").ap()
    scr_k = nc.dram_tensor("scr_k", [B, NG, PARTS, 32, S], BF16, kind="Internal").ap()
    scr_c = nc.dram_tensor("scr_c", [B, NG, PARTS, 32, SCP], BF16, kind="Internal").ap()

    ctx = ExitStack()
    with ctx:
        def sb(name, shape, dt=FP32):
            return ctx.enter_context(nc.sbuf_tensor(name, shape, dt))

        def sem(name):
            return ctx.enter_context(nc.semaphore(name))

        xT = sb("xT", [128, B, S])
        x_tok = sb("x_tok", [128, B, QT, D])
        ctxt = sb("ctxt", [128, B, SC])
        wa = sb("wa", [128, len(W_A), 128])
        wx = sb("wx", [128, len(W_X), 128])
        wg = sb("wg", [128, E])
        bcol = sb("bcol", [128, 6])
        brow = sb("brow", [128, 4, 128])
        c32 = sb("c32", [128, NC32])
        c16 = sb("c16", [128, NC16], BF16)
        qst = sb("qst", [KR, B, H, S], BF16)
        arena = sb("arena", [128, B, H, S], BF16)
        kst = arena[0:KR, :, :, :]
        kstc = sb("kstc", [KR, B, H, SCP], BF16)
        ab = sb("ab", [128, 2, 2, S])
        part = sb("part", [128, 2, PARTS, S], BF16)
        rest = sb("rest", [128, 2, S])
        partc = sb("partc", [128, PARTS, B, SCP], BF16)
        v_sb = sb("v_sb", [128, B, QT, H, 32])
        vc_sb = sb("vc_sb", [128, B, H, 32])
        vblk = sb("vblk", [128, B, NG, G, 32])
        negm = sb("negm", [128, 2, QT, G])
        mres = sb("mres", [128, 2, QT, G])
        mpart = sb("mpart", [128, 2, QT, PARTS, G], BF16)
        mrow = sb("mrow", [PARTS * G, 2, S], BF16)
        prob = sb("prob", [128, 2, G * (QT * (QT + 1) // 2) * 128])
        po_sb = sb("po_sb", [128, 2, S])
        rec = sb("rec", [128, 2, QT, G])
        onorm = sb("onorm", [128, QT, D])
        ot_sb = sb("ot_sb", [128, S])
        z = sb("z", [128, QT, D])
        stats = sb("stats", [128, QT, 6])
        mv = sb("mv", [128, QT, 2])
        rstd = sb("rstd", [128, QT])
        top = sb("top", [128, QT, 8])
        tix = sb("tix", [128, QT, 8], U32)
        gsm = sb("gsm", [128, 6, QT])
        gw = sb("gw", [128, 3, QT, E])
        gpart = sb("gpart", [128, QT, PARTS, E], BF16)
        gT = sb("gT", [PARTS * E, B, S], BF16)

        w1 = arena[:, 0, 0:8, :].rearrange("p a b -> p (a b)").bitcast(FP32)
        w3 = arena[:, 0, 8:16, :].rearrange("p a b -> p (a b)").bitcast(FP32)
        w2 = arena[:, 1, 0:8, :].rearrange("p a b -> p (a b)").bitcast(FP32)
        xg = prob[:, 0, 0:2 * S].rearrange("p (a t) -> p a t", a=2)
        silu = prob[:, 0, 2 * S:4 * S].rearrange("p (a t) -> p a t", a=2)
        gate = prob[:, 1, 0:4 * S].rearrange("p (a t) -> p a t", a=4)
        yT = prob[:, 1, 4 * S:5 * S]

        ident = c32[:, C_ID:C_ID + 128]
        iden16 = c16[:, H_ID:H_ID + 128]

        psA = [ctx.enter_context(nc.psum_tensor(f"psA{i}", [128, 512], FP32)) for i in range(2)]
        psB = [ctx.enter_context(nc.psum_tensor(f"psB{i}", [128, 512], FP32)) for i in range(2)]
        psO = [ctx.enter_context(nc.psum_tensor(f"psO{i}", [128, 512], FP32)) for i in range(2)]
        psJ = [ctx.enter_context(nc.psum_tensor(f"psJ{i}", [128, 512], FP32)) for i in range(2)]

        s_in = [sem(f"s_in{i}") for i in range(4)]
        s_tail = sem("s_tail")
        s_zero = sem("s_zero")
        s_xb = sem("s_xb")
        j_full = sem("j_full")
        j_done = [sem("j_done0"), sem("j_done1")]
        s_p1 = sem("s_p1")
        s_p2 = sem("s_p2")
        s_p3 = sem("s_p3")
        s_cp1 = sem("s_cp1")
        s_cp2 = sem("s_cp2")
        s_cres = sem("s_cres")
        s_cp3 = sem("s_cp3")
        s_sw = [sem(f"s_sw{i}") for i in range(7)]
        s_st = [[sem(f"s_st{a}_{g}") for g in range(NG)] for a in range(2 * B)]
        s_ck = sem("s_ck")
        s_a = sem("s_a")
        s_ar = sem("s_ar")
        s_mp = sem("s_mp")
        s_mr = [sem("s_mr0"), sem("s_mr1")]
        s_b = sem("s_b")
        s_e = sem("s_e")
        s_pv = sem("s_pv")
        s_po = sem("s_po")
        s_mv = sem("s_mv")
        s_rs = sem("s_rs")
        s_x = sem("s_x")
        s_gd = sem("s_gd")
        s_ge = sem("s_ge")
        s_gw = sem("s_gw")
        s_h1 = sem("s_h1")
        s_h3 = sem("s_h3")
        s_si = sem("s_si")
        s_gg = sem("s_gg")
        s_y = sem("s_y")
        s_yT = sem("s_yT")
        s_out = sem("s_out")
        s_dve = sem("s_dve")
        s_pool = sem("s_pool")

        block = ctx.enter_context(nc.Block())

        def job_done(eng, *item):
            n = JOB[(item[0], item[1:])] + JOBS[item[0]] - 1
            eng.wait_ge(j_done[n % 2], n // 2 + 1)

        def wait_stacks(eng, st, b, g):
            eng.wait_ge(s_st[2 * st + b][g], 16 * (6 if st == 0 else 3))
            if st == 1:
                eng.wait_ge(s_ck, 16 * B * PARTS)

        def prob_at(u, kt, j):
            if unit(u)[0] == 0:
                base = j * 1280 + [0, 512, 1024, 896][kt]
                return prob[:, u % 2, base:base + S - 128 * kt]
            n = j if kt == 0 else G
            return prob[:, u % 2, n * S:(n + 1) * S]

        @block.sync
        def _(sp):
            sp.dma_start(xT[:, :, :], xt_d).then_inc(s_in[0], 16)
            sp.dma_start(wa[:, 0:7, :], wa_d[:, 0:7, :]).then_inc(s_in[0], 16)
            sp.dma_start(c32[:, 0:2 * S], c32_d[:, 0:2 * S]).then_inc(s_in[0], 16)
            sp.dma_start(bcol[:, :], bcol_d).then_inc(s_in[0], 16)
            for b in range(B):
                for h in range(0, H, 8):
                    sp.dma_start(qst[ROWS:KR, b, h:h + 8, :],
                                 bass.AP(tail_d.tensor, 0, [[2 * S, KR - ROWS], [0, 8], [1, S]])).then_inc(s_tail, 16)
                    sp.dma_start(kst[ROWS:KR, b, h:h + 8, :],
                                 bass.AP(tail_d.tensor, S, [[2 * S, KR - ROWS], [0, 8], [1, S]])).then_inc(s_tail, 16)
            sp.dma_start(wa[:, 7:10, :], wa_d[:, 7:10, :]).then_inc(s_in[1], 16)
            sp.dma_start(ctxt[:, :, :], ctxt_d).then_inc(s_in[1], 16)
            sp.dma_start(wx[:, :, :], wx_d).then_inc(s_in[1], 16)
            sp.dma_start(wg[:, :], wg_d).then_inc(s_in[1], 16)
            sp.dma_start(c32[:, 2 * S:], c32_d[:, 2 * S:]).then_inc(s_in[1], 16)
            sp.dma_start(c16[:, :], c16_d).then_inc(s_in[1], 16)
            sp.dma_start(brow[:, :, :], bass.AP(brow_d.tensor, 0, [[0, 128], [1, 512]])).then_inc(s_in[1], 16)
            sp.dma_start(x_tok[:, :, :, :], x_d.rearrange("b (i p) d -> p b i d", p=128)).then_inc(s_in[3], 16)
            for b in range(B):
                for h in range(0, H, 8):
                    sp.dma_start(kstc[ROWS:KR, b, h:h + 8, :],
                                 bass.AP(tail_d.tensor, (KR - ROWS) * 2 * S, [[SCP, KR - ROWS], [0, 8], [1, SCP]])
                                 ).then_inc(s_tail, 16)

            def q_rows(st, b, g):
                for a in range(PARTS):
                    off = (((2 * st + b) * NG + g) * PARTS + a) * 32 * S
                    sp.dma_start(qst[PARTS * HD * a:PARTS * HD * (a + 1), b, G * g:G * g + G, :],
                                 bass.AP(scr_q.tensor, off, [[0, PARTS], [G * S, HD], [1, G * S]])
                                 ).then_inc(s_st[2 * st + b][g], 16)

            for kind, args in PLAN:
                if kind == "SPLIT":
                    b, w = args
                    n = 2 * b + (w == "k")
                    sp.wait_ge(s_p1, n + 1)
                    sp.wait_ge(s_p2, n + 1)
                    sp.wait_ge(s_p3, n + 1)
                    dst = (scr_k if w == "k" else scr_q)[b]
                    for a in range(PARTS):
                        sp.dma_start(dst[:, a, :, :], part[:, n % 2, a, :]).then_inc(s_sw[n], 16)
                elif kind == "STACK" and args[0] == 0:
                    _, b = args
                    sp.wait_ge(s_sw[2 * b], 16 * PARTS)
                    sp.wait_ge(s_sw[2 * b + 1], 16 * PARTS)
                    for g in range(NG):
                        q_rows(0, b, g)
                        for a in range(PARTS):
                            sp.dma_start(kst[PARTS * HD * a:PARTS * HD * (a + 1), b, G * g:G * g + G, :],
                                         bass.AP(scr_k.tensor, (b * NG + g) * PARTS * 32 * S, [[G * S, PARTS * HD], [1, G * S]])
                                         ).then_inc(s_st[b][g], 16)
                elif kind == "STACKCK":
                    sp.wait_ge(s_cp1, 1)
                    sp.wait_ge(s_cp2, 1)
                    sp.wait_ge(s_cp3, 1)
                    for b in range(B):
                        for a in range(PARTS):
                            sp.dma_start(scr_c[b, :, a, :, :], partc[:, a, b, :]).then_inc(s_sw[4], 16)
                    sp.wait_ge(s_sw[4], 16 * B * PARTS)
                    for b in range(B):
                        for a in range(PARTS):
                            dst = kstc[PARTS * HD * a:PARTS * HD * (a + 1), b, :, :].rearrange("p (g j) t -> p g (j t)", g=NG)
                            src = bass.AP(scr_c.tensor, b * NG * PARTS * 32 * SCP,
                                          [[G * SCP, PARTS * HD], [PARTS * 32 * SCP, NG], [1, G * SCP]])
                            sp.dma_start(dst, src).then_inc(s_ck, 16)
                elif kind == "STACK":
                    _, b = args
                    sp.wait_ge(s_cp1, b + 2)
                    sp.wait_ge(s_cp2, b + 2)
                    sp.wait_ge(s_cp3, b + 2)
                    for a in range(PARTS):
                        sp.dma_start(scr_q[2 + b][:, a, :, :], part[:, b, a, :]).then_inc(s_sw[5 + b], 16)
                    sp.wait_ge(s_e, b_base(NG * (b + 1)))
                    sp.dma_start(qst[ROWS:ROWS + PARTS, b, :, :],
                                 bass.AP(tail_d.tensor, 0, [[2 * S, PARTS], [0, H], [1, S]])).then_inc(s_sw[5 + b], 16)
                    sp.wait_ge(s_sw[5 + b], 16 * (PARTS + 1))
                    for g in range(NG):
                        q_rows(1, b, g)
                elif kind == "MT":
                    u, = args
                    st, b, g = unit(u)
                    job_done(sp, "MT", u)
                    sp.dma_start(qst[ROWS:ROWS + PARTS, b, G * g:G * g + G, :], mrow[:, u % 2, :]).then_inc(s_mr[u % 2], 16)
                    if u == NG * B + 1:
                        sp.wait_ge(s_e, b_base(2 * NG))
                        sp.dma_start(w1, w1_d).then_inc(s_in[2], 16)
                        sp.dma_start(w3, w3_d).then_inc(s_in[2], 16)
                        sp.dma_start(w2, w2_d).then_inc(s_in[2], 16)
                elif kind == "OUT":
                    b, = args
                    sp.wait_ge(s_x, 4 + b + 1)
                    sp.dma_start(out_d[b].rearrange("(i p) d -> p i d", p=128), x_tok[:, b, :, :]).then_inc(s_out, 16)
            sp.wait_ge(s_out, 16 * B)

        @block.gpsimd
        def _(pool):
            steps = [0]

            def link(ins):
                steps[0] += 1
                ins.then_inc(s_pool, 1)
                pool.wait_ge(s_pool, steps[0])

            link(nc.gpsimd.memset(partc[:, :, :, :], 0.0))
            link(nc.gpsimd.memset(v_sb[:, 0, :, :, :], 0.0))
            nc.gpsimd.memset(v_sb[:, 0, :, :, HD:HD + 1], 1.0).then_inc(s_zero, 1)
            pool.wait_ge(s_in[3], 16)
            pool.wait_ge(s_in[1], 16 * 7)
            nc.gpsimd.tensor_tensor(x_tok[:, :, :, :].rearrange("p b i d -> p (b i) d"),
                                    x_tok[:, :, :, :].rearrange("p b i d -> p (b i) d"),
                                    brow[:, 1:2, :].to_broadcast([128, B * QT, D]), ALU.add).then_inc(s_xb, 1)
            link(nc.gpsimd.memset(v_sb[:, 1, :, :, :], 0.0))
            nc.gpsimd.memset(v_sb[:, 1, :, :, HD:HD + 1], 1.0).then_inc(s_zero, 1)
            link(nc.gpsimd.memset(vc_sb[:, :, :, :], 0.0))
            nc.gpsimd.memset(vc_sb[:, :, :, HD:HD + 1], 1.0).then_inc(s_zero, 1)
            link(nc.gpsimd.memset(vblk[:, :, :, :, :], 0.0))
            for j in range(G):
                nc.gpsimd.memset(vblk[32 * j:32 * j + TAIL, :, :, j, HD:HD + 1], 1.0).then_inc(s_zero, 1)

            for kind, args in PLAN:
                if kind == "A":
                    u, k = args
                    if k < len(a_banks(u)) - 1:
                        continue
                    p = u % 2
                    pool.wait_ge(s_ar, a_base(u + 1))
                    if u >= 2:
                        job_done(pool, "MT", u - 2)
                    link(nc.gpsimd.tensor_copy(mpart[:, p, :, 0, :], negm[:, p, :, :]))
                    link(nc.gpsimd.tensor_tensor(mres[:, p, :, :], negm[:, p, :, :], mpart[:, p, :, 0, :], ALU.subtract))
                    link(nc.gpsimd.tensor_copy(mpart[:, p, :, 1, :], mres[:, p, :, :]))
                    nc.gpsimd.tensor_tensor(mpart[:, p, :, 2, :], mres[:, p, :, :], mpart[:, p, :, 1, :],
                                            ALU.subtract).then_inc(s_mp, 1)
                elif kind == "LN":
                    st, b = args
                    n = 2 * st + b
                    pool.wait_ge(s_mv, n + 1)
                    link(nc.gpsimd.tensor_scalar(mv[:, :, 1], mv[:, :, 1], EPS, None, ALU.add))
                    nc.gpsimd.tensor_tensor(rstd[:, :], mv[:, :, 1], c32[:, C_POW:C_POW + QT], ALU.pow).then_inc(s_rs, 1)

        @block.tensor
        def _(pe):
            def bank(n):
                if n >= 2:
                    pe.wait_ge(j_done[n % 2], n // 2)
                return psJ[n % 2]

            for item in PLAN:
                kind, args = item
                if kind == "U":
                    b, w = args
                    if b == 0 and w == "q":
                        pe.wait_ge(s_in[0], 16 * 4)
                    ps = bank(JOB[item])
                    nc.tensor.matmul(ps[:, :], wa[:, W_A["w" + w], :], xT[:, b, :], start=True, stop=True).then_inc(j_full, 1)
                elif kind == "H":
                    b, w = args
                    n = 3 * b + (w == "k")
                    ps = bank(JOB[item])
                    job_done(pe, "U", b, w)
                    nc.tensor.matmul(ps[:, :], wa[:, W_A["i" + w], :], ab[:, n % 2, 0, :], start=True, stop=False)
                    nc.tensor.matmul(ps[:, :], wa[:, W_A["i" + w + "s"], :], ab[:, n % 2, 1, :], start=False,
                                     stop=True).then_inc(j_full, 1)
                elif kind == "VH":
                    b, = args
                    n = 3 * b + 2
                    if b == 0:
                        pe.wait_ge(s_in[1], 16 * 7)
                    ps = bank(JOB[item])
                    job_done(pe, "U", b, "v")
                    for i in range(QT):
                        for half, w in enumerate(("iv", "ivs")):
                            last = nc.tensor.matmul(ps[:, 128 * i:128 * i + 128], ab[:, n % 2, half, 128 * i:128 * i + 128],
                                                    wa[:, W_A[w], :], start=half == 0, stop=half == 1)
                    last.then_inc(j_full, 1)
                elif kind == "CK":
                    for k, w in enumerate(("k", "ks")):
                        ps = bank(JOB[item] + k)
                        nc.tensor.matmul(ps[:, 0:B * SC], wx[:, W_X[w], :], ctxt[:, :, :].rearrange("p b t -> p (b t)"),
                                         start=True, stop=True).then_inc(j_full, 1)
                elif kind == "CV":
                    ps = bank(JOB[item])
                    for b in range(B):
                        nc.tensor.matmul(ps[:, 128 * b:128 * b + 128], ctxt[:, b, 0:128], wx[:, W_X["v"], :], start=True, stop=True)
                    for b in range(B):
                        for j in range(G):
                            last = nc.tensor.matmul(ps[32 * j:32 * j + TAIL, 128 * (B + b):128 * (B + b) + 128],
                                                    ctxt[:, b, 128:SC], wx[:, W_X["v"], :], start=True, stop=True)
                    last.then_inc(j_full, 1)
                elif kind == "A":
                    u, k = args
                    st, b, g = unit(u)
                    if k == 0:
                        wait_stacks(pe, st, b, g)
                        if u == 0:
                            pe.wait_ge(s_in[1], 16 * 7)
                            pe.wait_ge(s_tail, 16 * 12)
                    n = a_base(u) + k
                    if n >= 2:
                        pe.wait_ge(s_ar, n - 1)
                    ps = psA[n % 2]
                    blocks, width = a_banks(u)[k]
                    for m, (i, j) in enumerate(blocks):
                        h = G * g + j
                        keys = kst[:, b, h, 0:width] if st == 0 else kstc[:, b, h, 0:SC]
                        last = nc.tensor.matmul(ps[:, m * width:(m + 1) * width], qst[:, b, h, 128 * i:128 * i + 128], keys,
                                                start=m == 0, stop=st == 1 and m == len(blocks) - 1, skip_group_check=True)
                    if st == 0:
                        nb = len(blocks)
                        diag = ps[:, 0:nb * width].rearrange("p (m w) -> p m w", m=nb)[:, :, width - 128:width]
                        last = nc.tensor.matmul(diag, iden16, c16[:, H_MA:H_MA + 128].unsqueeze(1).to_broadcast([128, nb, 128]),
                                                start=False, stop=True, skip_group_check=True)
                    last.then_inc(s_a, 1)
                elif kind == "MT":
                    u, = args
                    ps = bank(JOB[item])
                    pe.wait_ge(s_mp, u + 1)
                    for i in range(QT):
                        last = nc.tensor.transpose(ps[0:PARTS * G, 64 * i:64 * i + 64].bitcast(BF16),
                                                   mpart[:, u % 2, i, :, :].rearrange("p a j -> p (a j)"), iden16)
                    last.then_inc(j_full, 1)
                elif kind == "B":
                    u, k = args
                    st, b, g = unit(u)
                    if k == 0:
                        pe.wait_ge(s_mr[u % 2], 16 * (u // 2 + 1))
                    n = b_base(u) + k
                    if n >= 2:
                        pe.wait_ge(s_e, n - 1)
                    ps = psB[n % 2]
                    blocks = b_banks(u)[k]
                    if st == 0:
                        for m, (kt, j, c) in enumerate(blocks):
                            h = G * g + j
                            nc.tensor.matmul(ps[:, c:c + S - 128 * kt], kst[:, b, h, 128 * kt:128 * kt + 128],
                                             qst[:, b, h, 128 * kt:S], start=m == 0, stop=False, skip_group_check=True)
                        if len(blocks) == 1:
                            diag, mask = ps[:, 0:128], c16[:, H_MB:H_MB + 128]
                        else:
                            step = blocks[1][2]
                            diag = bass.AP(ps[:, :].tensor, 0, [[512, 128], [step, 2], [1, 128]])
                            mask = c16[:, H_MB:H_MB + 128].unsqueeze(1).to_broadcast([128, 2, 128])
                        nc.tensor.matmul(diag, iden16, mask, start=False, stop=True, skip_group_check=True).then_inc(s_b, 1)
                    elif blocks[0][0] == 0:
                        h = G * g + blocks[0][1]
                        nc.tensor.matmul(ps[:, :], kstc[:, b, h, 0:128], qst[:, b, h, :], start=True, stop=True).then_inc(s_b, 1)
                    else:
                        for j in range(G):
                            h = G * g + j
                            last = nc.tensor.matmul(ps[32 * j:32 * j + 32, :], kstc[:, b, h, 128:SCP], qst[:, b, h, :],
                                                    start=True, stop=True)
                        last.then_inc(s_b, 1)
                elif kind == "PV":
                    u, kt = args
                    st, b, g = unit(u)
                    po = psO[u % 2]
                    if kt == 0:
                        if st == 0 and g == 0:
                            job_done(pe, "VH", b)
                        if st == 1 and b == 0 and g == 0:
                            job_done(pe, "CV")
                        if u >= 2:
                            pe.wait_ge(s_po, u - 1)
                    need = {0: 4, 1: 8, 3: 8, 2: 10}[kt] if st == 0 else 4 + kt
                    pe.wait_ge(s_e, b_base(u) + need)
                    if st == 0:
                        for j in range(G):
                            last = nc.tensor.matmul(po[32 * j:32 * j + 32, 128 * kt:S], v_sb[:, b, kt, G * g + j, :],
                                                    prob_at(u, kt, j), start=kt == 0, stop=kt == 2, skip_group_check=True)
                        if kt == 2:
                            last.then_inc(s_pv, 1)
                    elif kt == 0:
                        for j in range(G):
                            nc.tensor.matmul(po[32 * j:32 * j + 32, :], vc_sb[:, b, G * g + j, :], prob_at(u, 0, j),
                                             start=True, stop=False, skip_group_check=True)
                    else:
                        nc.tensor.matmul(po[:, :], vblk[:, b, g, :, :].rearrange("p j c -> p (j c)"), prob_at(u, 1, None),
                                         start=False, stop=True, skip_group_check=True).then_inc(s_pv, 1)
                elif kind == "OT":
                    u, = args
                    ps = bank(JOB[item])
                    pe.wait_ge(s_po, u + 1)
                    for i in range(QT):
                        last = nc.tensor.transpose(ps[:, 128 * i:128 * i + 128], po_sb[:, u % 2, 128 * i:128 * i + 128], ident)
                    last.then_inc(j_full, 1)
                elif kind == "ONT":
                    st, b = args
                    ps = bank(JOB[item])
                    job_done(pe, "OT", NG * (2 * st + b + 1) - 1)
                    for i in range(QT):
                        last = nc.tensor.transpose(ps[:, 128 * i:128 * i + 128], onorm[:, i, :], ident)
                    last.then_inc(j_full, 1)
                elif kind == "OP":
                    st, b = args
                    ps = bank(JOB[item])
                    job_done(pe, "ONT", st, b)
                    w = wa[:, W_A["out"], :] if st == 0 else wx[:, W_X["o"], :]
                    for i in range(QT):
                        last = nc.tensor.matmul(ps[:, 128 * i:128 * i + 128], ot_sb[:, 128 * i:128 * i + 128], w, start=True, stop=True)
                    last.then_inc(j_full, 1)
                elif kind == "XT":
                    st, b = args
                    ps = bank(JOB[item])
                    pe.wait_ge(s_x, 2 * st + b + 1)
                    for i in range(QT):
                        last = nc.tensor.transpose(ps[:, 128 * i:128 * i + 128], x_tok[:, b, i, :], ident)
                    last.then_inc(j_full, 1)
                elif kind == "CQ":
                    b, = args
                    job_done(pe, "XT", 0, b)
                    for k, w in enumerate(("q", "qs")):
                        ps = bank(JOB[item] + k)
                        nc.tensor.matmul(ps[:, :], wx[:, W_X[w], :], xT[:, b, :], start=True, stop=True).then_inc(j_full, 1)
                elif kind == "LG":
                    b, = args
                    ps = bank(JOB[item])
                    job_done(pe, "XT", 1, b)
                    for i in range(QT):
                        last = nc.tensor.matmul(ps[:, E * i:E * i + E], xT[:, b, 128 * i:128 * i + 128], wg[:, :], start=True, stop=True)
                    last.then_inc(j_full, 1)
                elif kind == "WT":
                    b, = args
                    ps = bank(JOB[item])
                    pe.wait_ge(s_gw, b + 1)
                    for i in range(QT):
                        last = nc.tensor.transpose(ps[0:PARTS * E, 64 * i:64 * i + 64].bitcast(BF16),
                                                   gpart[:, i, :, :].rearrange("p a e -> p (a e)"), iden16)
                    last.then_inc(j_full, 1)
                elif kind == "BC":
                    b, e = args
                    ps = bank(JOB[item])
                    job_done(pe, "WT", b)
                    nc.tensor.matmul(ps[:, :], c16[0:PARTS * E, H_SEL + 128 * e:H_SEL + 128 * e + 128], gT[:, b, :],
                                     start=True, stop=True).then_inc(j_full, 1)
                elif kind == "F1":
                    b, f = args
                    n = FT * b + f
                    if n == 0:
                        pe.wait_ge(s_in[2], 16 * 3)
                    if n < 2:
                        pe.wait_ge(s_ar, a_base(NU))
                        pe.wait_ge(s_e, b_base(NU))
                    else:
                        pe.wait_ge(s_si, n - 1)
                    nc.tensor.matmul(psA[n % 2][:, :], w1[:, 128 * f:128 * f + 128], xT[:, b, :], start=True, stop=True).then_inc(s_h1, 1)
                    if n >= 2:
                        pe.wait_ge(s_gg, n - 1)
                    job_done(pe, "BC", b, f // 2)
                    nc.tensor.matmul(psB[n % 2][:, :], w3[:, 128 * f:128 * f + 128], xg[:, (E * b + f // 2) % 2, :], start=True,
                                     stop=True).then_inc(s_h3, 1)
                elif kind == "F2":
                    b, f = args
                    n = FT * b + f
                    if f == 0:
                        pe.wait_ge(s_po, NU)
                    pe.wait_ge(s_gg, n + 1)
                    nc.tensor.matmul(psO[b][:, :], w2[:, 128 * f:128 * f + 128], gate[:, n % 4, :], start=f == 0,
                                     stop=f == FT - 1).then_inc(s_y, 1)
                elif kind == "YT":
                    b, = args
                    ps = bank(JOB[item])
                    pe.wait_ge(s_yT, b + 1)
                    for i in range(QT):
                        last = nc.tensor.transpose(ps[:, 128 * i:128 * i + 128], yT[:, 128 * i:128 * i + 128], ident)
                    last.then_inc(j_full, 1)

        @block.scalar
        def _(act):
            def bank(n):
                act.wait_ge(j_full, n + 1)
                return psJ[n % 2]

            def free(n, ins):
                ins.then_inc(j_done[n % 2], 1)

            for item in PLAN:
                kind, args = item
                if kind == "H":
                    b, w = args
                    n = 2 * b + (w == "k")
                    ps = bank(JOB[item])
                    if n >= 2:
                        act.wait_ge(s_sw[n - 2], 16 * PARTS)
                    nc.scalar.activation(part[:, n % 2, 0, :], ps[:, :], ACT.Identity, bias=bcol[:, n % 2:n % 2 + 1]).then_inc(s_p1, 1)
                    job_done(act, "H", b, w)
                    nc.scalar.activation(part[:, n % 2, 1, :], rest[:, n % 2, :], ACT.Copy).then_inc(s_p2, 1)
                elif kind == "CK":
                    act.wait_ge(s_cres, 1)
                    nc.scalar.activation(partc[:, 0, :, 0:SC], rest[:, 0, 0:B * SC].rearrange("p (b t) -> p b t", b=B),
                                         ACT.Copy).then_inc(s_cp1, 1)
                    act.wait_ge(s_cres, 2)
                    nc.scalar.activation(partc[:, 1, :, 0:SC], rest[:, 1, 0:B * SC].rearrange("p (b t) -> p b t", b=B),
                                         ACT.Copy).then_inc(s_cp2, 1)
                elif kind == "CQ":
                    b, = args
                    if b == 0:
                        act.wait_ge(s_sw[2], 16 * PARTS)
                        act.wait_ge(s_sw[3], 16 * PARTS)
                    act.wait_ge(s_cres, 2 * b + 3)
                    nc.scalar.activation(part[:, b, 0, :], rest[:, 0, :], ACT.Copy).then_inc(s_cp1, 1)
                    act.wait_ge(s_cres, 2 * b + 4)
                    nc.scalar.activation(part[:, b, 1, :], rest[:, 1, :], ACT.Copy).then_inc(s_cp2, 1)
                elif kind == "MT":
                    u, = args
                    ps = bank(JOB[item])
                    if u >= 2:
                        act.wait_ge(s_mr[u % 2], 16 * (u // 2))
                    free(JOB[item], nc.scalar.activation(mrow[:, u % 2, :], ps[0:PARTS * G, 0:256].bitcast(BF16), ACT.Copy))
                elif kind == "B":
                    u, k = args
                    st, b, g = unit(u)
                    n = b_base(u) + k
                    if k == 0 and u >= 2:
                        act.wait_ge(s_pv, u - 1)
                    act.wait_ge(s_b, n + 1)
                    ps = psB[n % 2]
                    if st == 0:
                        kt, j, _ = b_banks(u)[k][0]
                        if kt == 2:
                            dst = prob[:, u % 2, 1280 * j:1280 * (j + 2)].rearrange("p (j c) -> p j c", j=2)[:, :, 1024:1280]
                            src = ps[:, :].rearrange("p (j c) -> p j c", j=2)
                        elif kt == 1:
                            dst, src = prob[:, u % 2, 1280 * j + 512:1280 * j + 1024], ps[:, :]
                        else:
                            dst, src = prob_at(u, 0, j), ps[:, :]
                    else:
                        kt, j, _ = b_banks(u)[k][0]
                        dst, src = prob_at(u, kt, j), ps[:, :]
                    nc.scalar.activation(dst, src, ACT.Exp, scale=SCALE).then_inc(s_e, 1)
                elif kind == "POC":
                    u, = args
                    act.wait_ge(s_pv, u + 1)
                    if u >= 2:
                        job_done(act, "OT", u - 2)
                    nc.scalar.activation(po_sb[:, u % 2, :], psO[u % 2][:, :], ACT.Copy).then_inc(s_po, 1)
                elif kind == "ONT":
                    st, b = args
                    ps = bank(JOB[item])
                    if (st, b) != (0, 0):
                        job_done(act, "OP", *divmod(2 * st + b - 1, 2))
                    free(JOB[item], nc.scalar.activation(ot_sb[:, :], ps[:, :], ACT.Copy))
                elif kind == "XT":
                    st, b = args
                    ps = bank(JOB[item])
                    free(JOB[item], nc.scalar.activation(xT[:, b, :], ps[:, :], ACT.Copy))
                elif kind == "WT":
                    b, = args
                    ps = bank(JOB[item])
                    free(JOB[item], nc.scalar.activation(gT[:, b, :], ps[0:PARTS * E, 0:256].bitcast(BF16), ACT.Copy))
                elif kind == "GATE":
                    b, = args
                    act.wait_ge(s_gd, b + 1)
                    nc.scalar.activation(gsm[:, 3, :], gsm[:, 2, :], ACT.Exp).then_inc(s_ge, 1)
                elif kind == "F1":
                    b, f = args
                    n = FT * b + f
                    act.wait_ge(s_h1, n + 1)
                    if n == 0:
                        act.wait_ge(s_pv, NU)
                    if n >= 2:
                        act.wait_ge(s_gg, n - 1)
                    nc.scalar.activation(silu[:, n % 2, :], psA[n % 2][:, :], ACT.Silu).then_inc(s_si, 1)
                elif kind == "YE":
                    b, = args
                    act.wait_ge(s_y, FT * (b + 1))
                    if b == 1:
                        job_done(act, "YT", 0)
                    nc.scalar.activation(yT, psO[b][:, :], ACT.Copy).then_inc(s_yT, 1)

        @block.vector
        def _(dve):
            steps = [0]

            def link(ins):
                steps[0] += 1
                ins.then_inc(s_dve, 1)
                dve.wait_ge(s_dve, steps[0])

            def bank(n):
                dve.wait_ge(j_full, n + 1)
                return psJ[n % 2]

            def free(n, ins):
                ins.then_inc(j_done[n % 2], 1)

            for item in PLAN:
                kind, args = item
                if kind == "U":
                    b, w = args
                    n = 3 * b + "qkv".index(w)
                    if n == 0:
                        dve.wait_ge(s_in[0], 16 * 4)
                    ps = bank(JOB[item])
                    if n >= 2:
                        before = [i for i in PLAN if i[0] in ("H", "VH")][n - 2]
                        dve.wait_ge(j_full, JOB[before] + 1)
                    nc.vector.tensor_tensor(ab[:, n % 2, 0, :], ps[:, :], c32[:, C_CA:C_CA + S], ALU.mult)
                    free(JOB[item], nc.vector.tensor_tensor(ab[:, n % 2, 1, :], ps[:, :], c32[:, C_SA:C_SA + S], ALU.mult))
                elif kind == "H":
                    b, w = args
                    n = 2 * b + (w == "k")
                    ps = bank(JOB[item])
                    dve.wait_ge(s_p1, n + 1)
                    nc.vector.scalar_tensor_tensor(out=rest[:, n % 2, :], in0=ps[:, :], scalar=bcol[:, n % 2:n % 2 + 1],
                                                   in1=part[:, n % 2, 0, :], op0=ALU.add, op1=ALU.subtract).then_inc(j_done[JOB[item] % 2], 1)
                    job_done(dve, *("H", b, w))
                    dve.wait_ge(s_p2, n + 1)
                    nc.vector.tensor_tensor(part[:, n % 2, 2, :], rest[:, n % 2, :], part[:, n % 2, 1, :], ALU.subtract).then_inc(s_p3, 1)
                elif kind == "VH":
                    b, = args
                    ps = bank(JOB[item])
                    dve.wait_ge(s_zero, b + 1)
                    dve.wait_ge(s_in[1], 16 * 7)
                    tiles = lambda x: x.rearrange("p (i h d) -> p i h d", i=QT, h=H)
                    bias = brow[:, 0, :].rearrange("p (h d) -> p h d", h=H).unsqueeze(1).to_broadcast([128, QT, H, HD])
                    free(JOB[item], nc.vector.tensor_tensor(v_sb[:, b, :, :, 0:HD], tiles(ps[:, :]), bias, ALU.add))
                elif kind == "CK":
                    n = JOB[item]
                    tw = lambda x: x.rearrange("p (b t) -> p b t", b=B)
                    for k, c in enumerate((C_CK, C_SK)):
                        ps = bank(n + k)
                        if k == 0:
                            dve.wait_ge(s_p2, 2 * B)
                            dve.wait_ge(s_p3, 2 * B)
                        ins = nc.vector.scalar_tensor_tensor(out=tw(rest[:, k, 0:B * SC]), in0=tw(ps[:, 0:B * SC]), scalar=bcol[:, 4 + k:5 + k],
                                                             in1=c32[:, c:c + SC].unsqueeze(1).to_broadcast([128, B, SC]), op0=ALU.add, op1=ALU.mult)
                        free(n + k, ins)
                    dve.wait_ge(j_done[n % 2], n // 2 + 1)
                    dve.wait_ge(j_done[(n + 1) % 2], (n + 1) // 2 + 1)
                    nc.vector.tensor_tensor(rest[:, 0, 0:B * SC], rest[:, 0, 0:B * SC], rest[:, 1, 0:B * SC], ALU.add).then_inc(s_cres, 1)
                    dve.wait_ge(s_cres, 1)
                    dve.wait_ge(s_cp1, 1)
                    dve.wait_ge(s_zero, 1)
                    nc.vector.tensor_tensor(tw(rest[:, 1, 0:B * SC]), tw(rest[:, 0, 0:B * SC]), partc[:, 0, :, 0:SC], ALU.subtract).then_inc(s_cres, 1)
                    dve.wait_ge(s_cres, 2)
                    dve.wait_ge(s_cp2, 1)
                    nc.vector.tensor_tensor(partc[:, 2, :, 0:SC], tw(rest[:, 1, 0:B * SC]), partc[:, 1, :, 0:SC], ALU.subtract).then_inc(s_cp3, 1)
                elif kind == "CV":
                    ps = bank(JOB[item])
                    dve.wait_ge(s_zero, 3 + G)
                    heads = lambda x: x.rearrange("p (h d) -> p h d", h=H)
                    for b in range(B):
                        nc.vector.tensor_tensor(vc_sb[:, b, :, 0:HD], heads(ps[:, 128 * b:128 * b + 128]), heads(brow[:, 2, :]), ALU.add)
                    for b in range(B):
                        for j in range(G):
                            rows = slice(32 * j, 32 * j + TAIL)
                            pick = lambda x: x.rearrange("p (g j d) -> p g j d", g=NG, j=G)[:, :, j, :]
                            last = nc.vector.tensor_tensor(vblk[rows, b, :, j, 0:HD], pick(ps[rows, 128 * (B + b):128 * (B + b) + 128]),
                                                           pick(brow[rows, 2, :]), ALU.add)
                    free(JOB[item], last)
                elif kind == "A":
                    u, k = args
                    n = a_base(u) + k
                    blocks, width = a_banks(u)[k]
                    dve.wait_ge(s_a, n + 1)
                    if k == 0 and u >= 2:
                        dve.wait_ge(s_mp, u - 1)
                    nb = len(blocks)
                    c = blocks[0][0] * G + blocks[0][1]
                    nc.vector.tensor_reduce(negm[:, u % 2, :, :].rearrange("p i j -> p (i j)")[:, c:c + nb],
                                            psA[n % 2][:, 0:nb * width].rearrange("p (m w) -> p m w", m=nb), AX.X, ALU.max,
                                            negate=True).then_inc(s_ar, 1)
                elif kind == "OT":
                    u, = args
                    st, b, g = unit(u)
                    ps = bank(JOB[item])
                    if g == 0 and u > 0:
                        job_done(dve, "ONT", *divmod(u // NG - 1, 2))
                    o = ps[:, :].rearrange("p (i j c) -> p i j c", i=QT, j=G)
                    link(nc.vector.reciprocal(rec[:, u % 2, :, :], o[:, :, :, HD]))
                    ins = nc.vector.tensor_tensor(onorm[:, :, 32 * g:32 * g + 32].rearrange("p i (j d) -> p i j d", j=G), o[:, :, :, 0:HD],
                                                  rec[:, u % 2, :, :].unsqueeze(3).to_broadcast([128, QT, G, HD]), ALU.mult)
                    free(JOB[item], ins)
                elif kind in ("OP", "YT"):
                    st, b = args if kind == "OP" else (2, args[0])
                    ps = bank(JOB[item])
                    if st == 0:
                        dve.wait_ge(s_xb, 1)
                    res = x_tok[:, b, :, :]
                    ins = nc.vector.tensor_tensor(z[:, :, :], ps[:, :].rearrange("p (i d) -> p i d", i=QT), res, ALU.add)
                    free(JOB[item], ins)
                    dve.wait_ge(j_done[JOB[item] % 2], JOB[item] // 2 + 1)
                    if st == 1:
                        link(nc.vector.tensor_tensor(z[:, :, :], z[:, :, :], brow[:, 3:4, :].to_broadcast([128, QT, D]), ALU.add))
                elif kind == "LN":
                    st, b = args
                    n = 2 * st + b
                    for i in range(QT):
                        last = nc.vector.bn_stats(stats[:, i, :], z[:, i, :])
                    link(last)
                    for i in range(QT):
                        last = nc.vector.bn_aggr(mv[:, i, :], stats[:, i, :])
                    last.then_inc(s_mv, 1)
                    dve.wait_ge(s_rs, n + 1)
                    for i in range(QT):
                        last = nc.vector.tensor_scalar(x_tok[:, b, i, :], z[:, i, :], mv[:, i, 0:1], rstd[:, i:i + 1], ALU.subtract, ALU.mult)
                    last.then_inc(s_x, 1)
                elif kind == "CQ":
                    b, = args
                    n = JOB[item]
                    for k, c in enumerate((C_CQ, C_SQ)):
                        ps = bank(n + k)
                        if k == 0:
                            dve.wait_ge(s_cp2, b + 1)
                        ins = nc.vector.scalar_tensor_tensor(out=rest[:, k, :], in0=ps[:, :], scalar=bcol[:, 2 + k:3 + k],
                                                             in1=c32[:, c:c + S], op0=ALU.add, op1=ALU.mult)
                        free(n + k, ins)
                    dve.wait_ge(j_done[n % 2], n // 2 + 1)
                    dve.wait_ge(j_done[(n + 1) % 2], (n + 1) // 2 + 1)
                    nc.vector.tensor_tensor(rest[:, 0, :], rest[:, 0, :], rest[:, 1, :], ALU.add).then_inc(s_cres, 1)
                    dve.wait_ge(s_cres, 2 * b + 3)
                    dve.wait_ge(s_cp1, b + 2)
                    nc.vector.tensor_tensor(rest[:, 1, :], rest[:, 0, :], part[:, b, 0, :], ALU.subtract).then_inc(s_cres, 1)
                    dve.wait_ge(s_cres, 2 * b + 4)
                    dve.wait_ge(s_cp2, b + 2)
                    nc.vector.tensor_tensor(part[:, b, 2, :], rest[:, 1, :], part[:, b, 1, :], ALU.subtract).then_inc(s_cp3, 1)
                elif kind == "GATE":
                    b, = args
                    job = JOB[("LG", (b,))]
                    ps = bank(job)
                    lg = ps[:, 0:QT * E].rearrange("p (i e) -> p i e", i=QT)
                    for i in range(QT):
                        last = nc.vector.max(top[:, i, :], lg[:, i, :])
                    link(last)
                    for i in range(QT):
                        last = nc.vector.max_index(tix[:, i, :], top[:, i, :], lg[:, i, :])
                    free(job, last)
                    dve.wait_ge(j_done[job % 2], job // 2 + 1)
                    first, second = gsm[:, 0, :], gsm[:, 1, :]
                    link(nc.vector.tensor_copy(first, tix[:, :, 0]))
                    link(nc.vector.tensor_copy(second, tix[:, :, 1]))
                    nc.vector.tensor_tensor(gsm[:, 2, :], top[:, :, 1], top[:, :, 0], ALU.subtract).then_inc(s_gd, 1)
                    dve.wait_ge(s_ge, b + 1)
                    link(nc.vector.tensor_scalar(gsm[:, 4, :], gsm[:, 3, :], 1.0, None, ALU.add))
                    link(nc.vector.reciprocal(gsm[:, 4, :], gsm[:, 4, :]))
                    link(nc.vector.tensor_tensor(gsm[:, 5, :], gsm[:, 3, :], gsm[:, 4, :], ALU.mult))
                    full = lambda x: x.unsqueeze(2).to_broadcast([128, QT, E])
                    iota = c32[:, C_IOTA:C_IOTA + E].unsqueeze(1).to_broadcast([128, QT, E])
                    link(nc.vector.tensor_tensor(gw[:, 0, :, :], iota, full(first), ALU.is_equal))
                    link(nc.vector.tensor_tensor(gw[:, 0, :, :], gw[:, 0, :, :], full(gsm[:, 4, :]), ALU.mult))
                    link(nc.vector.tensor_tensor(gw[:, 1, :, :], iota, full(second), ALU.is_equal))
                    link(nc.vector.tensor_tensor(gw[:, 1, :, :], gw[:, 1, :, :], full(gsm[:, 5, :]), ALU.mult))
                    link(nc.vector.tensor_tensor(gw[:, 0, :, :], gw[:, 0, :, :], gw[:, 1, :, :], ALU.add))
                    if b > 0:
                        job_done(dve, "WT", b - 1)
                    link(nc.vector.tensor_copy(gpart[:, :, 0, :], gw[:, 0, :, :]))
                    link(nc.vector.tensor_tensor(gw[:, 2, :, :], gw[:, 0, :, :], gpart[:, :, 0, :], ALU.subtract))
                    link(nc.vector.tensor_copy(gpart[:, :, 1, :], gw[:, 2, :, :]))
                    nc.vector.tensor_tensor(gpart[:, :, 2, :], gw[:, 2, :, :], gpart[:, :, 1, :], ALU.subtract).then_inc(s_gw, 1)
                elif kind == "BC":
                    b, e = args
                    n = E * b + e
                    ps = bank(JOB[item])
                    if n == 0:
                        dve.wait_ge(s_pv, NU)
                    if n >= 2:
                        dve.wait_ge(s_h3, 2 * (n - 1))
                    ins = nc.vector.tensor_tensor(xg[:, n % 2, :], ps[:, :], xT[:, b, :], ALU.mult)
                    free(JOB[item], ins)
                elif kind == "F1":
                    b, f = args
                    n = FT * b + f
                    dve.wait_ge(s_si, n + 1)
                    dve.wait_ge(s_h3, n + 1)
                    if n >= 4:
                        dve.wait_ge(s_y, n - 3)
                    nc.vector.tensor_tensor(gate[:, n % 4, :], psB[n % 2][:, :], silu[:, n % 2, :], ALU.mult).then_inc(s_gg, 1)


_ATTN_Q = [8 * (4 * (p // 32) + p % 4) + p % 32 // 4 for p in range(128)]


def constants():
    f = np.float32
    i = np.arange(D // 2, dtype=f)
    theta = (10000.0 ** (-2.0 * (i.astype(np.float64) - 1.0) / D)).astype(f)
    ang = np.arange(S, dtype=f)[:, None] * theta[None, :]
    c, s = np.cos(ang).astype(f), np.sin(ang).astype(f)
    c32 = np.zeros((128, NC32), f)
    c32[:, C_CA:C_CA + S] = np.repeat(c, 2, axis=1).T
    sa = np.repeat(s, 2, axis=1).T.copy()
    sa[0::2] *= -1
    c32[:, C_SA:C_SA + S] = sa

    inv = (1.0 / 10000.0 ** (np.arange(0, HD, 2, dtype=np.float64) / HD)).astype(f)
    dim = np.arange(128) % 32 // 4
    sign = np.where(dim < HD // 2, -1, 1).astype(f)[:, None]
    for n, cc, cs in ((S, C_CQ, C_SQ), (SC, C_CK, C_SK)):
        t = np.arange(n, dtype=f)
        fr = np.outer(f(10.0) * (t / f(n)), inv).astype(f)
        c32[:, cc:cc + n] = np.cos(fr).astype(f).T[dim % (HD // 2)]
        c32[:, cs:cs + n] = np.sin(fr).astype(f).T[dim % (HD // 2)] * sign
    c32[:, C_ID:C_ID + 128] = np.eye(128)
    c32[:, C_IOTA:C_IOTA + E] = np.arange(E)
    c32[:, C_POW:C_POW + QT] = -0.5
    bf = np.dtype("bfloat16")
    c16 = np.zeros((128, NC16), f)
    c16[:, H_ID:H_ID + 128] = np.eye(128)
    q, k = np.arange(128)[:, None], np.arange(128)[None, :]
    c16[:, H_MA:H_MA + 128] = np.where(k > q, NEG, 0)
    c16[:, H_MB:H_MB + 128] = np.where(q > k, NEG, 0)
    for e in range(E):
        for a in range(PARTS):
            c16[E * a + e, H_SEL + 128 * e:H_SEL + 128 * e + 128] = 1
    tail = np.zeros((KR - ROWS, 2, S), f)
    tail[:PARTS, 1] = 1
    tailc = np.zeros((KR - ROWS, SCP), f)
    tailc[:PARTS, :SC] = 1
    return c32, c16.astype(bf), np.concatenate([tail.ravel(), tailc.ravel()]).astype(bf)


def kernel(**inputs):
    import concourse.bacc as bacc
    from concourse.bass_utils import run_bass_kernel_spmd as run

    a = {k: np.asarray(v) for k, v in inputs.items()}
    order, swap2, swap4 = np.array(_ATTN_Q), np.arange(D) ^ 1, np.arange(D) ^ 4
    ip, ib = a["L0_attn_in_proj_w"], a["L0_attn_in_proj_b"]
    iq, ik, iv = ip[0:D], ip[D:2 * D], ip[2 * D:3 * D]
    wa = [a["L0_attn_wq"].T, a["L0_attn_wk"].T, a["L0_attn_wv"].T,
          iq[order].T, iq[order].T[swap2], ik[order].T, ik[order].T[swap2], iv.T, iv.T[swap2], a["L0_attn_out_w"].T]
    xq, xk = a["L0_xattn_Wq"], a["L0_xattn_Wk"]
    wx = [xq[order].T, xq[swap4][order].T, xk[order].T, xk[swap4][order].T, a["L0_xattn_Wv"].T, a["L0_xattn_Wo"].T]
    bq, bk = a["L0_xattn_bq"], a["L0_xattn_bk"]
    bcol = [ib[0:D][order], ib[D:2 * D][order], bq[order], bq[swap4][order], bk[order], bk[swap4][order]]
    brow = [ib[2 * D:], a["L0_attn_out_b"], a["L0_xattn_bv"], a["L0_xattn_bo"]]
    c32, c16, tail = constants()
    arrays = {
        "xt": a["x"].transpose(2, 0, 1), "x": a["x"], "ctxt": a["ctx_1024"].transpose(2, 0, 1),
        "wa": np.stack(wa, axis=1), "wx": np.stack(wx, axis=1), "wg": a["L0_ffn_wg"].T,
        "bcol": np.stack(bcol, axis=1), "brow": np.concatenate(brow),
        "c32": c32, "c16": c16, "tail": tail,
        "w1": a["L0_ffn_w1"].reshape(E * I, D).T, "w3": a["L0_ffn_w3"].reshape(E * I, D).T,
        "w2": a["L0_ffn_w2"].transpose(0, 2, 1).reshape(FT, 128, D).transpose(1, 0, 2).reshape(128, FT * D),
    }
    arrays = {k: np.ascontiguousarray(v) for k, v in arrays.items()}
    nc = bacc.Bacc("TRN2", target_bir_lowering=False, num_devices=1)
    args = [nc.dram_tensor(k + "_dram", v.shape, mybir.dt.from_np(v.dtype), kind="ExternalInput").ap() for k, v in arrays.items()]
    out = nc.dram_tensor("out_dram", (B, S, D), FP32, kind="ExternalOutput").ap()
    layer_kernel(nc, *args, out)
    r = run(nc, [{k + "_dram": v for k, v in arrays.items()}], core_ids=[0])
    return r.results[0]["out_dram"]
```

```python
import numpy as np

import concourse.bass as bass
from concourse import mybir
from contextlib import ExitStack

FP32 = mybir.dt.float32
BF16 = mybir.dt.bfloat16
FP32R = mybir.dt.float32r
U32 = mybir.dt.uint32
ALU = mybir.AluOpType
ACT = mybir.ActivationFunctionType
AX = mybir.AxisListType

B, S, D = 2, 512, 128
SC = 154
H, HD = 16, 8
G = 4
NG = H // G
QT = S // 128
E, I = 8, 256
FT = E * I // 128
WC = 4
PARTS = 3
ROWS = PARTS * PARTS * HD
KR = 96
SCP = 160
TAIL = SC - 128
NEG = -1e30
SCALE = float(np.float32(HD) ** np.float32(-0.5))
EPS = 1e-5
NU = 2 * B * NG

W_A = {n: i for i, n in enumerate(["wq", "wk", "wv", "iq", "iqs", "ik", "iks", "iv", "ivs", "out"])}
W_X = {n: i for i, n in enumerate(["q", "qs", "k", "ks", "v", "o"])}
C_CA, C_SA, C_CQ, C_SQ = 0, S, 2 * S, 3 * S
C_CK, C_SK = 4 * S, 4 * S + SC
C_ID = 4 * S + 2 * SC
C_IOTA = C_ID + 128
C_POW = C_IOTA + E
NC32 = C_POW + QT
H_ID, H_MA, H_MB, H_SEL = 0, 128, 256, 384
NC16 = H_SEL + E * 128


def unit(u):
    return u // (B * NG), u // NG % B, u % NG


def a_banks(u):
    if unit(u)[0] == 0:
        out = []
        for i in range(QT):
            n = min(G, QT // (i + 1)) if i < 2 else 1
            for j in range(0, G, n):
                out.append(([(i, j + k) for k in range(n)], 128 * (i + 1)))
        return out
    blocks = [(i, j) for i in range(QT) for j in range(G)]
    return [(blocks[k:k + 3], SC) for k in range(0, QT * G, 3)]


def b_banks(u):
    if unit(u)[0] == 0:
        out = [[(0, j, 0)] for j in range(G)]
        out += [[(1, j, 0), (3, j, S - 128)] for j in range(G)]
        out += [[(2, j, 0), (2, j + 1, 256)] for j in range(0, G, 2)]
        return out
    return [[(0, j, 0)] for j in range(G)] + [[(1, None, 0)]]


def po_bank(u):
    return u % 2 if u < NU - NG else 1


def masks(u, kt):
    return 2 * QT * u + {0: 2, 1: 4, 3: 6, 2: 8}[kt]


LEAD = {
    "U": 0.29,
    "CK": 0.43,
    "A": 0.27,
    "MT": 0.24,
    "B": 0.3,
    "MK": 0.62,
    "PV": 0.11,
    "POC": 0.98,
    "OT": 0.46,
    "ONT": 0.52,
    "CQ": 0.46,
    "LG": 0.51,
    "WS": 0.19,
    "BC": 0.1,
    "F": 0.24,
    "F3": -0.07,
    "F2": -0.04,
}
IDLE_COST = 0.01
LATENCY = 0.21
AHEAD = 3
F3_WAIT = 4.47


def make_plan():
    free = {e: 0.0 for e in ("PE", "ACT", "DVE", "POOL", "SP")}
    done, plan = {}, []

    streams = []

    def stream(name):
        streams.append([])
        items = streams[-1]
        return lambda item, stages, deps=(), after=0.0, late=(): items.append((name, item, stages, list(deps), after, list(late)))

    add = stream("U")
    add(("WARM", (10,)), [("PE", 5.6)])
    for w in "qk":
        add(("U", (0, w)), [("PE", 1.7), ("DVE", 1.2, -1.3)])
    for w in "qk":
        add(("H", (0, w)), [("PE", 1.7), ("ACT", 0.6), ("DVE", 0.66)], [("U", (0, w))])
    add(("U", (0, "v")), [("PE", 0.9)])
    add(("WARM", (9,)), [("PE", 2.0)])
    for w in "qk":
        add(("H2", (0, w)), [("ACT", 0.48), ("DVE", 0.6)])
        add(("SPLIT", (0, w)), [("SP", 1.65)], [("H2", (0, w))], 2.0)
    add(("TURN", ()), [("DVE", 1.2)])
    add(("VH", (0,)), [("PE", 1.7), ("DVE", 0.6)])
    for g in range(NG):
        add(("STACK", (0, 0, g)), [("SP", 2.2)], [("SPLIT", (0, "q")), ("SPLIT", (0, "k"))], 2.2)
    add(("TAIL", ()), [("SP", 2.2)])
    add = stream("U")
    for n, w in enumerate("qk"):
        add(("U", (1, w)), [("PE", 0.86), ("DVE", 1.2)], [("VH", (0,))])
    for n, w in enumerate("qk"):
        add(("H", (1, w)), [("PE", 1.71), ("ACT", 0.6), ("DVE", 0.66)], [("U", (1, w)), ("SPLIT", (0, w))])
        add(("H2", (1, w)), [("ACT", 0.48), ("DVE", 0.6)])
        add(("SPLIT", (1, w)), [("SP", 1.65)], [("H2", (1, w))], 2.0)
    for g in range(NG):
        add(("STACK", (0, 1, g)), [("SP", 2.2)], [("SPLIT", (1, "q")), ("SPLIT", (1, "k"))], 2.2)
    add(("U", (1, "v")), [("PE", 0.86), ("DVE", 1.2)])
    add(("VH", (1,)), [("PE", 1.71), ("DVE", 0.6)], [("U", (1, "v"))])
    add = stream("CK")
    add(("CK", ()), [("PE", 1.03), ("DVE", 1.3, -0.3), ("ACT", 0.35)], [("VH", (1,))])
    add(("CK2", ()), [("DVE", 0.4), ("ACT", 0.35)], [("CK", ())])
    add(("CK3", ()), [("DVE", 0.4)], [("CK2", ())])
    add(("STACKCK", ()), [("SP", 9.0)], [("CK3", ())], 2.2)
    add(("CV", ()), [("PE", 0.98), ("DVE", 1.22)])

    row = lambda u: (u // NG // B, u // NG % B)
    last_b = lambda u: ("B", (u, len(b_banks(u)) - 1))
    last_pv = lambda u: ("PV", (u, 2 if unit(u)[0] == 0 else 1))
    add = stream("A")
    for u in range(NU):
        st, b, g = unit(u)
        for k, (blocks, width) in enumerate(a_banks(u)):
            cols = len(blocks) * (width + (128 if st == 0 else 0))
            stages = [("PE", cols / 2400.0), ("DVE", 0.12 + len(blocks) * width / 1050.0)]
            if k == len(a_banks(u)) - 1:
                stages.append(("POOL", 1.0))
            deps = [("STACK", (st, b, g))] if k == 0 else []
            if k == 0 and st == 1:
                deps.append(("STACKCK", ()))
            if k == 0 and u >= NG:
                deps.append(("B", (u - AHEAD, 0)))
            add(("A", (u, k)), stages, deps)
    add = stream("MT")
    for u in range(NU):
        add(("MT", (u,)), [("PE", 0.21), ("ACT", 0.6)], [("A", (u, len(a_banks(u)) - 1))], 2.3)
    add = stream("B")
    for u in range(NU):
        for k in range(len(b_banks(u))):
            late = [(1, last_pv(u - 2))] if u >= 2 else []
            add(("B", (u, k)), [("PE", 0.25), ("ACT", 0.48)], [("MT", (u,))], 0.0, late)
    add = stream("MK")
    for u in range(B * NG):
        for kt, k in ((0, 3), (1, 7), (3, 7), (2, 9)):
            add(("MK", (u, kt)), [("POOL", 0.72)], [("B", (u, k))])
    add = stream("PV")
    for u in range(NU):
        st, b, g = unit(u)
        if st == 0:
            for kt, us in ((0, 0.92), (1, 0.7), (3, 0.28), (2, 0.49)):
                deps = [("MK", (u, kt)), ("VH", (b,))]
                if u >= 2:
                    deps.append(("POC", (u - 2,)))
                add(("PV", (u, kt)), [("PE", us)], deps)
        else:
            for kt, us in ((0, 0.92), (1, 0.87)):
                add(("PV", (u, kt)), [("PE", us)], [("B", (u, 3 + kt)), ("CV", ()), ("POC", (u - (2 if u < NU - NG else 1),))])
    add = stream("POC")
    for u in range(NU):
        add(("POC", (u,)), [("ACT", 0.48)], [last_pv(u)] + ([("OT", (u - 2,))] if u >= 2 else []))
    add = stream("OT")
    for u in range(NU):
        deps = [("POC", (u,))]
        if u % NG == 0 and u > 0:
            deps.append(("ONT", row(u - 1)))
        add(("OT", (u,)), [("PE", 0.43), ("DVE", 0.55)], deps)
    for n in range(2 * B):
        st, b = divmod(n, B)
        add = stream("ONT")
        add(("ONT", (st, b)), [("PE", 0.43), ("ACT", 0.48)],
            [("OT", (NG * (n + 1) - 1,))] + ([("OP", divmod(n - 1, B))] if n else []))
        add(("OP", (st, b)), [("PE", 0.86), ("DVE", 0.6 + 0.65 * st)],
            [("ONT", (st, b))] + ([("LNX", divmod(n - 1, B))] if n else []))
        add(("LN", (st, b)), [("DVE", 1.1), ("POOL", 1.3)], [("OP", (st, b))])
        add(("LNX", (st, b)), [("DVE", 1.02)], [("LN", (st, b))])
        if st == 0:
            add(("XT", (st, b)), [("PE", 0.43), ("ACT", 0.48)], [("LNX", (st, b))])
            add = stream("CQ")
            add(("CQ", (b,)), [("PE", 1.71), ("DVE", 1.93, -0.66), ("ACT", 0.52)],
                [("XT", (st, b)), ("CK3", ()) if b == 0 else ("CQ3", (0,))])
            add(("CQ2", (b,)), [("DVE", 0.6), ("ACT", 0.52)], [("CQ", (b,))])
            add(("CQ3", (b,)), [("DVE", 0.6)], [("CQ2", (b,))])
            for g in range(NG):
                add(("STACK", (1, b, g)), [("SP", 5.0 if g == 0 else 1.65)], [("CQ3", (b,)), last_b(NG * (b + 1) - 1)], 2.2)
        else:
            add(("XT", (st, b)), [("PE", 0.43), ("ACT", 0.96), ("DVE", 0.6, -0.3)], [("LNX", (st, b))])
            add = stream("LG")
            add(("LG", (b,)), [("PE", 1.2)], [("XT", (st, b))] + ([("WT", (0,))] if b else []))
            add(("GATE", (b,)), [("DVE", 1.3), ("ACT", 0.1)], [("LG", (b,))])
            add(("GATE2", (b,)), [("DVE", 0.6)], [("GATE", (b,))])
            add(("GATE3", (b,)), [("DVE", 2.2)], [("GATE2", (b,))])
            add(("WT", (b,)), [("PE", 0.21), ("ACT", 0.48)], [("GATE3", (b,)), ("STACK", (1, 1, 0))])

    add = stream("WS")
    for c in range(2 * WC):
        add(("WD", (c,)), [("SP", 0.55)], [("WS", (c - 2,))] if c >= 2 else [last_pv(2)], 2.3)
        if c == 0:
            add(("W2", ()), [("SP", 0.55)], [last_pv(NG - 1)], 2.3)
    add = stream("WS")
    for c in range(2 * WC):
        add(("WS", (c,)), [("ACT", 0.52), ("POOL", 1.23)], [("WD", (c,)), last_b(NG * (c // WC + 1) - 1)])
    tile = lambda n: divmod(n, FT)
    add = stream("BC")
    for n in range(B * E):
        b, e = divmod(n, E)
        add(("BC", (b, e)), [("PE", 0.21), ("ACT", 0.48)],
            [("WT", (b,)), last_pv(B * NG - 1)] + ([("F1", tile(2 * (n - 1) - 1))] if n >= 2 else []))
    add = stream("F")
    for n in range(B * FT):
        b, f = tile(n)
        deps, late = [("XT", (1, b)), ("BC", (b, f // 2)), ("WS", (WC - 1,))], []
        if n >= 2:
            late = [(1, ("F1", tile(n - 2))), (3, ("F3", tile(n - 2)))]
        add(("F1", (b, f)), [("PE", 0.65), ("ACT", 0.48), ("DVE", 0.6), ("POOL", 1.23)], deps, 0.0, late)
    add = stream("F3")
    for n in range(B * FT):
        late = [(1, ("F1", tile(n)))]
        if n >= 4:
            late.append((1, ("F2", tile(n - 4))))
        add(("F3", tile(n)), [("PE", 0.65), ("DVE", 0.6)], [("WS", (2 * WC - 1,))], 0.0, late)
    add = stream("F2")
    for n in range(B * FT):
        deps = [("F3", tile(n)), ("POC", (NU - NG - 2 if n < FT else NU - 1,)), ("W2", ())]
        add(("F2", tile(n)), [("PE", 0.86)], deps)
    add = stream("F2")
    for b in range(B):
        add(("YE", (b,)), [("ACT", 0.48)], [("F2", (b, FT - 1)), ("OP", (1, 1))] + ([("YT", (0,))] if b else []))
        add(("YT", (b,)), [("PE", 0.43), ("DVE", 0.6)], [("YE", (b,)), ("LNX", (1, 1) if b == 0 else (2, 0))])
        add(("LN", (2, b)), [("DVE", 1.1), ("POOL", 1.3)], [("YT", (b,))])
        add(("LNX", (2, b)), [("DVE", 1.02)], [("LN", (2, b))])
        add(("OUT", (b,)), [("SP", 0.5)], [("LNX", (2, b))])

    banks = {ring: [] for ring in RINGS}
    heads = [0] * len(streams)
    while True:
        best = None
        for i, items in enumerate(streams):
            if heads[i] == len(items):
                continue
            name, item, stages, deps, after, late = items[heads[i]]
            if any(d not in done for d in deps + [d for _, d in late]):
                continue
            ready = max([done[d] + LATENCY for d in deps] + [0.0])
            for ring, kinds in RINGS.items():
                if item[0] in kinds and len(banks[ring]) >= 2:
                    ready = max(ready, banks[ring][-2] + LATENCY)
            t, ends, idle = ready, [], 0.0
            for n, stage in enumerate(stages):
                engine, us, lag = (stage + (LATENCY,))[:3]
                t = max([t] + [done[d] for m, d in late if m == n])
                begin = max(free[engine], t + (lag if n else 0.0))
                if n:
                    idle += max(0.0, begin - max(free[engine], start))
                else:
                    start = begin
                t = begin + us
                ends.append(t)
            if item[0] == "F3":
                start = max(start, done[("F1", item[1])] - F3_WAIT)
            score = start - LEAD[name] + IDLE_COST * idle
            if name == "U" and item[1] and item[1][0] == 0:
                score = -1.0
            if best is None or score < best[0]:
                best = (score, i, item, stages, ends, after)
        if best is None:
            break
        _, i, item, stages, ends, after = best
        heads[i] += 1
        for stage, end in zip(stages, ends):
            free[stage[0]] = end
        done[item] = ends[-1] + after
        for ring, kinds in RINGS.items():
            if item[0] in kinds:
                read = ends[2] if item[0] == "F1" else ends[min(1, len(ends) - 1)]
                banks[ring] += [read] * kinds[item[0]]
        if item[0] != "TURN":
            plan.append(item)
    assert all(heads[i] == len(items) for i, items in enumerate(streams)), "an input is never planned"
    return plan


RINGS = {
    "J": {"U": 1, "H": 1, "VH": 1, "CK": 2, "CV": 1, "MT": 1, "OT": 1, "ONT": 1, "OP": 1, "XT": 1,
          "CQ": 2, "LG": 1, "WT": 1, "BC": 1, "YT": 1},
    "A": {"A": 1, "F1": 1},
    "B": {"B": 1, "F3": 1},
}


PLAN = make_plan()


def fill_numbers(kinds):
    numbers, n = {}, 0
    for item in PLAN:
        if item[0] in kinds:
            numbers[item] = n
            n += kinds[item[0]]
    return numbers


FILL = {ring: fill_numbers(kinds) for ring, kinds in RINGS.items()}
JOB = FILL["J"]


def layer_kernel(nc, xt_d, x_d, ctxt_d, wa_d, wx_d, wg_d, bcol_d, brow_d, c32_d, c16_d, tail_d, w1_d, w3_d, w2_d, out_d):
    scr_q = nc.dram_tensor("scr_q", [2 * B, NG, PARTS, 32, S], BF16, kind="Internal").ap()
    scr_k = nc.dram_tensor("scr_k", [B, NG, PARTS, 32, S], BF16, kind="Internal").ap()
    scr_c = nc.dram_tensor("scr_c", [B, NG, PARTS, 32, SCP], BF16, kind="Internal").ap()

    ctx = ExitStack()
    with ctx:
        def sb(name, shape, dt=FP32):
            return ctx.enter_context(nc.sbuf_tensor(name, shape, dt))

        def sem(name):
            return ctx.enter_context(nc.semaphore(name))

        xT = sb("xT", [128, B, S])
        x_tok = sb("x_tok", [128, B, QT, D])
        ctxt = sb("ctxt", [128, B, SC])
        wa = sb("wa", [128, len(W_A), 128])
        wx = sb("wx", [128, len(W_X), 128])
        wg = sb("wg", [128, E])
        bcol = sb("bcol", [128, 6])
        brow = sb("brow", [128, 4, 128])
        c32 = sb("c32", [128, NC32])
        c16 = sb("c16", [128, NC16], BF16)
        qst = sb("qst", [KR, B, H, S], BF16)
        kst = []
        wparts = []
        for b in range(B):
            early = nc.sbuf_tensor(f"kst{b}", [KR, H, S], BF16)
            kst.append(early.__enter__())
            early.__exit__(None, None, None)
            wparts.append([sb(f"w{2 * b + 1}{p}", [128, FT * 128], FP32R) for p in ("high", "low")])
        kstc = sb("kstc", [KR, B, H, SCP], BF16)
        early = nc.sbuf_tensor("ab", [128, 2, 2, S], FP32)
        ab = early.__enter__()
        early.__exit__(None, None, None)
        x_high = sb("x_high", [128, B, S], FP32R)
        x_low = sb("x_low", [128, B, S], FP32R)
        part = sb("part", [128, 2, PARTS, S], BF16)
        rest = sb("rest", [128, 2, S])
        partc = sb("partc", [128, PARTS, B, SCP], BF16)
        early = nc.sbuf_tensor("v0", [128, QT, H, 32], FP32)
        v_sb = [early.__enter__()]
        early.__exit__(None, None, None)
        w2 = sb("w2", [128, FT * 128])
        v_sb.append(sb("v1", [128, QT, H, 32]))
        vc_sb = sb("vc_sb", [128, B, H, 32])
        vblk = sb("vblk", [128, B, NG, G, 32])
        negm = sb("negm", [128, 2, QT, G])
        mres = sb("mres", [128, 2, QT, G])
        mpart = sb("mpart", [128, 2, QT, PARTS, G], BF16)
        mrow = sb("mrow", [PARTS * G, 2, S], BF16)
        prob = sb("prob", [128, 2, 5 * S])
        early = nc.sbuf_tensor("prob_more", [128, 2, 5 * S], FP32)
        prob_more = early.__enter__()
        early.__exit__(None, None, None)
        silu = sb("silu", [128, 2, S])
        gated = sb("gated", [128, 2, S])
        wbc = sb("wbc", [128, 2, S])
        hid = sb("hid", [128, 4, S])
        stage = sb("stage", [128, 2, FT * 128 // WC])
        po_sb = sb("po_sb", [128, 2, S])
        rec = sb("rec", [128, 2, QT, G])
        onorm = sb("onorm", [128, QT, D])
        ot_sb = sb("ot_sb", [128, S])
        z = sb("z", [128, QT, D])
        stats = sb("stats", [128, QT, 6])
        mv = sb("mv", [128, QT, 2])
        rstd = sb("rstd", [128, QT])
        top = sb("top", [128, QT, 8])
        tix = sb("tix", [128, QT, 8], U32)
        gsm = sb("gsm", [128, 6, QT])
        gw = sb("gw", [128, 3, QT, E])
        gpart = sb("gpart", [128, QT, PARTS, E], BF16)
        gT = part[0:PARTS * E, 0, 0:B, :]

        yT = ot_sb[:, :]

        ident = c32[:, C_ID:C_ID + 128]
        iden16 = c16[:, H_ID:H_ID + 128]

        psA = [ctx.enter_context(nc.psum_tensor(f"psA{i}", [128, 512], FP32)) for i in range(2)]
        psB = [ctx.enter_context(nc.psum_tensor(f"psB{i}", [128, 512], FP32)) for i in range(2)]
        psO = [ctx.enter_context(nc.psum_tensor(f"psO{i}", [128, 512], FP32)) for i in range(2)]
        psJ = [ctx.enter_context(nc.psum_tensor(f"psJ{i}", [128, 512], FP32)) for i in range(2)]

        s_first = sem("s_first")
        s_rest = sem("s_rest")
        s_xtok = sem("s_xtok")
        s_iq = sem("s_iq")
        s_iv = sem("s_iv")
        s_turn = sem("s_turn")
        s_row = sem("s_row")
        s_x1 = sem("s_x1")
        s_tail = [sem(f"s_tail{i}") for i in range(B + 1)]
        s_zero = sem("s_zero")
        s_xb = sem("s_xb")
        j_full = sem("j_full")
        j_done = [sem("j_done0"), sem("j_done1")]
        s_p1 = sem("s_p1")
        s_p2 = sem("s_p2")
        s_p3 = sem("s_p3")
        s_cp1 = sem("s_cp1")
        s_cp2 = sem("s_cp2")
        s_cp3 = sem("s_cp3")
        s_cres = sem("s_cres")
        s_sw = [sem(f"s_sw{i}") for i in range(7)]
        s_st = [[sem(f"s_st{a}_{g}") for g in range(NG)] for a in range(2 * B)]
        s_ck = sem("s_ck")
        s_a = sem("s_a")
        a_done = [sem("a_done0"), sem("a_done1")]
        s_mp = sem("s_mp")
        s_mr = [sem("s_mr0"), sem("s_mr1")]
        s_b = sem("s_b")
        b_done = [sem("b_done0"), sem("b_done1")]
        s_mk = sem("s_mk")
        s_pv = sem("s_pv")
        s_po = sem("s_po")
        s_mv = sem("s_mv")
        s_rs = sem("s_rs")
        s_x = sem("s_x")
        s_gd = sem("s_gd")
        s_ge = sem("s_ge")
        s_gw = sem("s_gw")
        s_wd = [sem("s_wd0"), sem("s_wd1")]
        s_w2 = sem("s_w2")
        s_wh = sem("s_wh")
        s_wl = sem("s_wl")
        s_xh = sem("s_xh")
        s_sg = sem("s_sg")
        s_th = sem("s_th")
        s_y = sem("s_y")
        s_yT = sem("s_yT")
        s_out = sem("s_out")
        s_dve = sem("s_dve")
        s_pool = sem("s_pool")

        block = ctx.enter_context(nc.Block())

        def job_done(eng, *item):
            n = JOB[(item[0], item[1:])] + RINGS["J"][item[0]] - 1
            eng.wait_ge(j_done[n % 2], n // 2 + 1)

        def fill_done(eng, ring, items):
            done = a_done if ring == "A" else b_done
            last = {}
            for item in items:
                n = FILL[ring][item]
                last[n % 2] = max(last.get(n % 2, 0), n // 2 + 1)
            for parity, count in sorted(last.items()):
                eng.wait_ge(done[parity], count)

        def exps_done(eng, u, banks):
            fill_done(eng, "B", [("B", (u, k)) for k in banks])

        def wait_stacks(eng, st, b, g):
            eng.wait_ge(s_st[2 * st + b][g], 16 * (PARTS + 1 if st == 0 else PARTS))
            if st == 0:
                eng.wait_ge(s_tail[b], 16 * 2)
            else:
                eng.wait_ge(s_ck, 16 * B * PARTS)
                eng.wait_ge(s_tail[B], 16 * B)

        def prob_at(u, kt, j):
            if unit(u)[0] == 0:
                half = (prob, prob_more)[j // 2]
                base = j % 2 * 1280 + [0, 512, 1024, 896][kt]
                return half[:, u % 2, base:base + S - 128 * kt]
            n = j if kt == 0 else G
            return prob[:, u % 2, n * S:(n + 1) * S]

        @block.sync
        def _(sp):
            def tails(b):
                sp.dma_start(qst[ROWS:KR, b, :, :],
                             bass.AP(tail_d.tensor, 0, [[2 * S, KR - ROWS], [0, H], [1, S]])).then_inc(s_tail[b], 16)
                sp.dma_start(kst[b][ROWS:KR, :, :],
                             bass.AP(tail_d.tensor, S, [[2 * S, KR - ROWS], [0, H], [1, S]])).then_inc(s_tail[b], 16)

            sp.dma_start(xT[:, 0, :], xt_d[:, 0, :]).then_inc(s_first, 16)
            sp.dma_start(wa[:, 3:7, :], wa_d[:, 3:7, :]).then_inc(s_iq, 16)
            sp.dma_start(xT[:, 1, :], xt_d[:, 1, :]).then_inc(s_x1, 16)
            tails(0)

            def q_rows(st, b, g):
                for a in range(PARTS):
                    off = (((2 * st + b) * NG + g) * PARTS + a) * 32 * S
                    sp.dma_start(qst[PARTS * HD * a:PARTS * HD * (a + 1), b, G * g:G * g + G, :],
                                 bass.AP(scr_q.tensor, off, [[0, PARTS], [G * S, HD], [1, G * S]])
                                 ).then_inc(s_st[2 * st + b][g], 16)

            def k_rows(b, g):
                off = (b * NG + g) * PARTS * 32 * S
                sp.dma_start(kst[b][0:ROWS, G * g:G * g + G, :],
                             bass.AP(scr_k.tensor, off, [[0, PARTS], [G * S, PARTS * HD], [1, G * S]])
                             ).then_inc(s_st[b][g], 16)

            for kind, args in PLAN:
                if kind == "TAIL":
                    tails(1)
                    for b in range(B):
                        sp.dma_start(kstc[ROWS:KR, b, :, :],
                                     bass.AP(tail_d.tensor, (KR - ROWS) * 2 * S, [[SCP, KR - ROWS], [0, H], [1, SCP]])
                                     ).then_inc(s_tail[B], 16)
                elif kind == "SPLIT":
                    b, w = args
                    n = 2 * b + (w == "k")
                    dst = (scr_k if w == "k" else scr_q)[b]
                    for a, ready in enumerate((s_p1, s_p2, s_p3)):
                        sp.wait_ge(ready, n + 1)
                        sp.dma_start(dst[:, a, :, :], part[:, n % 2, a, :]).then_inc(s_sw[n], 16)
                elif kind == "STACK" and args[0] == 0:
                    _, b, g = args
                    if g == 0:
                        sp.wait_ge(s_sw[2 * b], 16 * PARTS)
                    q_rows(0, b, g)
                    if g == 0:
                        sp.wait_ge(s_sw[2 * b + 1], 16 * PARTS)
                    k_rows(b, g)
                elif kind == "STACKCK":
                    sp.wait_ge(s_cp1, 1)
                    sp.wait_ge(s_cp2, 1)
                    sp.wait_ge(s_cp3, 1)
                    for b in range(B):
                        for a in range(PARTS):
                            sp.dma_start(scr_c[b, :, a, :, :], partc[:, a, b, :]).then_inc(s_sw[4], 16)
                    sp.wait_ge(s_sw[4], 16 * B * PARTS)
                    for b in range(B):
                        for a in range(PARTS):
                            dst = kstc[PARTS * HD * a:PARTS * HD * (a + 1), b, :, :].rearrange("p (g j) t -> p g (j t)", g=NG)
                            src = bass.AP(scr_c.tensor, b * NG * PARTS * 32 * SCP,
                                          [[G * SCP, PARTS * HD], [PARTS * 32 * SCP, NG], [1, G * SCP]])
                            sp.dma_start(dst, src).then_inc(s_ck, 16)
                elif kind == "STACK":
                    _, b, g = args
                    if g == 0:
                        for a, ready in enumerate((s_cp1, s_cp2, s_cp3)):
                            sp.wait_ge(ready, b + 2)
                            sp.dma_start(scr_q[2 + b][:, a, :, :], part[:, b, a, :]).then_inc(s_sw[5 + b], 16)
                        exps_done(sp, NG * (b + 1) - 1, range(len(b_banks(0))))
                        sp.dma_start(qst[ROWS:ROWS + PARTS, b, :, :],
                                     bass.AP(tail_d.tensor, 0, [[2 * S, PARTS], [0, H], [1, S]])).then_inc(s_sw[5 + b], 16)
                        sp.wait_ge(s_sw[5 + b], 16 * (PARTS + 1))
                    q_rows(1, b, g)
                elif kind == "WD":
                    c, = args
                    if c >= 2:
                        sp.wait_ge(s_wl, c - 1)
                    cols = slice(c % WC * (FT * 128 // WC), (c % WC + 1) * (FT * 128 // WC))
                    sp.dma_start(stage[:, c % 2, :], (w1_d, w3_d)[c // WC][:, cols]).then_inc(s_wd[c % 2], 16)
                elif kind == "W2":
                    sp.wait_ge(s_pv, NG)
                    sp.dma_start(w2[:, :], w2_d).then_inc(s_w2, 16)
                elif kind == "OUT":
                    b, = args
                    sp.wait_ge(s_x, 4 + b + 1)
                    sp.dma_start(out_d[b].rearrange("(i p) d -> p i d", p=128), x_tok[:, b, :, :]).then_inc(s_out, 16)
            sp.wait_ge(s_out, 16 * B)

        @block.gpsimd
        def _(pool):
            steps = [0]

            def link(ins):
                steps[0] += 1
                ins.then_inc(s_pool, 1)
                pool.wait_ge(s_pool, steps[0])

            link(nc.gpsimd.memset(partc[:, :, :, :], 0.0))
            pool.dma_start(brow[:, :, :], bass.AP(brow_d.tensor, 0, [[0, 128], [1, 512]])).then_inc(s_row, 16)
            pool.dma_start(x_tok[:, :, :, :], x_d.rearrange("b (i p) d -> p b i d", p=128)).then_inc(s_xtok, 16)
            link(nc.gpsimd.memset(v_sb[0][:, :, :, :], 0.0))
            nc.gpsimd.memset(v_sb[0][:, :, :, HD:HD + 1], 1.0).then_inc(s_zero, 1)
            pool.wait_ge(s_xtok, 16)
            pool.wait_ge(s_row, 16)
            nc.gpsimd.tensor_tensor(x_tok[:, :, :, :].rearrange("p b i d -> p (b i) d"),
                                    x_tok[:, :, :, :].rearrange("p b i d -> p (b i) d"),
                                    brow[:, 1:2, :].to_broadcast([128, B * QT, D]), ALU.add).then_inc(s_xb, 1)
            link(nc.gpsimd.memset(v_sb[1][:, :, :, :], 0.0))
            nc.gpsimd.memset(v_sb[1][:, :, :, HD:HD + 1], 1.0).then_inc(s_zero, 1)
            link(nc.gpsimd.memset(vc_sb[:, :, :, :], 0.0))
            nc.gpsimd.memset(vc_sb[:, :, :, HD:HD + 1], 1.0).then_inc(s_zero, 1)
            link(nc.gpsimd.memset(vblk[:, :, :, :, :], 0.0))
            for j in range(G):
                nc.gpsimd.memset(vblk[32 * j:32 * j + TAIL, :, :, j, HD:HD + 1], 1.0).then_inc(s_zero, 1)
                pool.wait_ge(s_zero, 3 + j + 1)

            for kind, args in PLAN:
                if kind == "A":
                    u, k = args
                    if k < len(a_banks(u)) - 1:
                        continue
                    p = u % 2
                    fill_done(pool, "A", [("A", (u, i)) for i in range(k + 1)])
                    if u >= 2:
                        job_done(pool, "MT", u - 2)
                    link(nc.gpsimd.tensor_copy(mpart[:, p, :, 0, :], negm[:, p, :, :]))
                    link(nc.gpsimd.tensor_tensor(mres[:, p, :, :], negm[:, p, :, :], mpart[:, p, :, 0, :], ALU.subtract))
                    link(nc.gpsimd.tensor_copy(mpart[:, p, :, 1, :], mres[:, p, :, :]))
                    nc.gpsimd.tensor_tensor(mpart[:, p, :, 2, :], mres[:, p, :, :], mpart[:, p, :, 1, :],
                                            ALU.subtract).then_inc(s_mp, 1)
                elif kind == "MK":
                    u, kt = args
                    exps_done(pool, u, {0: range(4), 1: range(4, 8), 3: range(4, 8), 2: range(8, 10)}[kt])
                    base = [0, 512, 1024, 896][kt]
                    for half in (prob, prob_more):
                        diag = half[:, u % 2, :].rearrange("p (j c) -> p j c", j=2)[:, :, base:base + 128]
                        nc.gpsimd.affine_select(out=diag, in_=diag, pattern=[[0, 2], [1, 128]], compare_op=ALU.is_ge, fill=0.0,
                                                base=0, channel_multiplier=-1).then_inc(s_mk, 1)
                elif kind == "WS":
                    c, = args
                    cols = slice(c % WC * (FT * 128 // WC), (c % WC + 1) * (FT * 128 // WC))
                    pool.wait_ge(s_wh, c + 1)
                    nc.gpsimd.tensor_tensor(wparts[c // WC][1][:, cols], stage[:, c % 2, :], wparts[c // WC][0][:, cols].bitcast(FP32),
                                            ALU.subtract).then_inc(s_wl, 1)
                elif kind == "F1":
                    b, f = args
                    n = FT * b + f
                    fill_done(pool, "A", [("F1", (b, f))])
                    job_done(pool, "BC", b, f // 2)
                    if n >= 2:
                        fill_done(pool, "B", [("F3", divmod(n - 2, FT))])
                    nc.gpsimd.tensor_tensor(gated[:, n % 2, :], silu[:, n % 2, :], wbc[:, (E * b + f // 2) % 2, :],
                                            ALU.mult).then_inc(s_sg, 1)
                elif kind == "LN":
                    st, b = args
                    n = 2 * st + b
                    pool.wait_ge(s_mv, n + 1)
                    link(nc.gpsimd.tensor_scalar(mv[:, :, 1], mv[:, :, 1], EPS, None, ALU.add))
                    nc.gpsimd.tensor_tensor(rstd[:, :], mv[:, :, 1], c32[:, C_POW:C_POW + QT], ALU.pow).then_inc(s_rs, 1)

        @block.tensor
        def _(pe):
            def bank(n):
                if n >= 2:
                    pe.wait_ge(j_done[n % 2], n // 2)
                return psJ[n % 2]

            def ring_bank(ring, item):
                n = FILL[ring][item]
                banks, done = (psA, a_done) if ring == "A" else (psB, b_done)
                if n >= 2:
                    pe.wait_ge(done[n % 2], n // 2)
                return banks[n % 2]

            def three_products(ps, w, b, f):
                cols = slice(128 * f, 128 * f + 128)
                high, low = w
                nc.tensor.matmul(ps[:, :], high[:, cols], x_high[:, b, :], start=True, stop=False)
                nc.tensor.matmul(ps[:, :], high[:, cols], x_low[:, b, :], start=False, stop=False)
                return nc.tensor.matmul(ps[:, :], low[:, cols], x_high[:, b, :], start=False, stop=True)

            for item in PLAN:
                kind, args = item
                if kind == "WARM":
                    count, = args
                    pe.wait_ge(s_pool, 1)
                    for _ in range(int(count)):
                        nc.tensor.matmul(psO[1][:, 0:B * SCP], partc[:, 0, 0, 0:128], partc[:, 0, :, :], start=True, stop=True)
                elif kind == "U":
                    b, w = args
                    if w == "q":
                        if b == 0:
                            pe.wait_ge(s_first, 16 * 2)
                        else:
                            pe.wait_ge(s_x1, 16)
                    ps = bank(JOB[item])
                    nc.tensor.matmul(ps[:, :], wa[:, W_A["w" + w], :], xT[:, b, :], start=True, stop=True).then_inc(j_full, 1)
                elif kind == "H":
                    b, w = args
                    n = 3 * b + (w == "k")
                    ps = bank(JOB[item])
                    if n == 0:
                        pe.wait_ge(s_iq, 16 * 2)
                    job_done(pe, "U", b, w)
                    nc.tensor.matmul(ps[:, :], wa[:, W_A["i" + w], :], ab[:, n % 2, 0, :], start=True, stop=False)
                    nc.tensor.matmul(ps[:, :], wa[:, W_A["i" + w + "s"], :], ab[:, n % 2, 1, :], start=False,
                                     stop=True).then_inc(j_full, 1)
                elif kind == "VH":
                    b, = args
                    n = 3 * b + 2
                    if b == 0:
                        pe.wait_ge(s_iv, 16)
                    ps = bank(JOB[item])
                    job_done(pe, "U", b, "v")
                    for i in range(QT):
                        for half, w in enumerate(("iv", "ivs")):
                            last = nc.tensor.matmul(ps[:, 128 * i:128 * i + 128], ab[:, n % 2, half, 128 * i:128 * i + 128],
                                                    wa[:, W_A[w], :], start=half == 0, stop=half == 1)
                    last.then_inc(j_full, 1)
                elif kind == "CK":
                    for k, w in enumerate(("k", "ks")):
                        ps = bank(JOB[item] + k)
                        nc.tensor.matmul(ps[:, 0:B * SC], wx[:, W_X[w], :], ctxt[:, :, :].rearrange("p b t -> p (b t)"),
                                         start=True, stop=True).then_inc(j_full, 1)
                elif kind == "CV":
                    ps = bank(JOB[item])
                    for b in range(B):
                        nc.tensor.matmul(ps[:, 128 * b:128 * b + 128], ctxt[:, b, 0:128], wx[:, W_X["v"], :], start=True, stop=True)
                    for b in range(B):
                        for j in range(G):
                            last = nc.tensor.matmul(ps[32 * j:32 * j + TAIL, 128 * (B + b):128 * (B + b) + 128],
                                                    ctxt[:, b, 128:SC], wx[:, W_X["v"], :], start=True, stop=True)
                    last.then_inc(j_full, 1)
                elif kind == "A":
                    u, k = args
                    st, b, g = unit(u)
                    if k == 0:
                        wait_stacks(pe, st, b, g)
                        if u == 0:
                            pe.wait_ge(s_rest, 16 * 5)
                    ps = ring_bank("A", item)
                    blocks, width = a_banks(u)[k]
                    for m, (i, j) in enumerate(blocks):
                        h = G * g + j
                        keys = kst[b][:, h, 0:width] if st == 0 else kstc[:, b, h, 0:SC]
                        last = nc.tensor.matmul(ps[:, m * width:(m + 1) * width], qst[:, b, h, 128 * i:128 * i + 128], keys,
                                                start=m == 0, stop=st == 1 and m == len(blocks) - 1, skip_group_check=True)
                    if st == 0:
                        nb = len(blocks)
                        diag = ps[:, 0:nb * width].rearrange("p (m w) -> p m w", m=nb)[:, :, width - 128:width]
                        last = nc.tensor.matmul(diag, iden16, c16[:, H_MA:H_MA + 128].unsqueeze(1).to_broadcast([128, nb, 128]),
                                                start=False, stop=True, skip_group_check=True)
                    last.then_inc(s_a, 1)
                elif kind == "MT":
                    u, = args
                    ps = bank(JOB[item])
                    pe.wait_ge(s_mp, u + 1)
                    for i in range(QT):
                        last = nc.tensor.transpose(ps[0:PARTS * G, 64 * i:64 * i + 64].bitcast(BF16),
                                                   mpart[:, u % 2, i, :, :].rearrange("p a j -> p (a j)"), iden16)
                    last.then_inc(j_full, 1)
                elif kind == "B":
                    u, k = args
                    st, b, g = unit(u)
                    if k == 0:
                        pe.wait_ge(s_mr[u % 2], 16 * (u // 2 + 1))
                    ps = ring_bank("B", item)
                    blocks = b_banks(u)[k]
                    if st == 0:
                        for m, (kt, j, c) in enumerate(blocks):
                            h = G * g + j
                            last = nc.tensor.matmul(ps[:, c:c + S - 128 * kt], kst[b][:, h, 128 * kt:128 * kt + 128],
                                                    qst[:, b, h, 128 * kt:S], start=m == 0, stop=m == len(blocks) - 1,
                                                    skip_group_check=True)
                        last.then_inc(s_b, 1)
                    elif blocks[0][0] == 0:
                        h = G * g + blocks[0][1]
                        nc.tensor.matmul(ps[:, :], kstc[:, b, h, 0:128], qst[:, b, h, :], start=True, stop=True).then_inc(s_b, 1)
                    else:
                        for j in range(G):
                            h = G * g + j
                            last = nc.tensor.matmul(ps[32 * j:32 * j + 32, :], kstc[:, b, h, 128:SCP], qst[:, b, h, :],
                                                    start=True, stop=True)
                        last.then_inc(s_b, 1)
                elif kind == "PV":
                    u, kt = args
                    st, b, g = unit(u)
                    po = psO[po_bank(u)]
                    if kt == 0:
                        if st == 0 and g == 0:
                            job_done(pe, "VH", b)
                        if st == 1 and b == 0 and g == 0:
                            job_done(pe, "CV")
                        if u >= 2:
                            pe.wait_ge(s_po, u - 1 if u < NU - NG else u)
                    if st == 0:
                        pe.wait_ge(s_mk, masks(u, kt))
                    else:
                        exps_done(pe, u, range(4) if kt == 0 else [4])
                    if st == 0:
                        for j in range(G):
                            last = nc.tensor.matmul(po[32 * j:32 * j + 32, 128 * kt:S], v_sb[b][:, kt, G * g + j, :],
                                                    prob_at(u, kt, j), start=kt == 0, stop=kt == 2, skip_group_check=True)
                        if kt == 2:
                            last.then_inc(s_pv, 1)
                    elif kt == 0:
                        for j in range(G):
                            nc.tensor.matmul(po[32 * j:32 * j + 32, :], vc_sb[:, b, G * g + j, :], prob_at(u, 0, j),
                                             start=True, stop=False, skip_group_check=True)
                    else:
                        nc.tensor.matmul(po[:, :], vblk[:, b, g, :, :].rearrange("p j c -> p (j c)"), prob_at(u, 1, None),
                                         start=False, stop=True, skip_group_check=True).then_inc(s_pv, 1)
                elif kind == "OT":
                    u, = args
                    ps = bank(JOB[item])
                    pe.wait_ge(s_po, u + 1)
                    for i in range(QT):
                        last = nc.tensor.transpose(ps[:, 128 * i:128 * i + 128], po_sb[:, u % 2, 128 * i:128 * i + 128], ident)
                    last.then_inc(j_full, 1)
                elif kind == "ONT":
                    st, b = args
                    ps = bank(JOB[item])
                    job_done(pe, "OT", NG * (2 * st + b + 1) - 1)
                    for i in range(QT):
                        last = nc.tensor.transpose(ps[:, 128 * i:128 * i + 128], onorm[:, i, :], ident)
                    last.then_inc(j_full, 1)
                elif kind == "OP":
                    st, b = args
                    ps = bank(JOB[item])
                    job_done(pe, "ONT", st, b)
                    w = wa[:, W_A["out"], :] if st == 0 else wx[:, W_X["o"], :]
                    for i in range(QT):
                        last = nc.tensor.matmul(ps[:, 128 * i:128 * i + 128], ot_sb[:, 128 * i:128 * i + 128], w, start=True, stop=True)
                    last.then_inc(j_full, 1)
                elif kind == "XT":
                    st, b = args
                    ps = bank(JOB[item])
                    pe.wait_ge(s_x, 2 * st + b + 1)
                    for i in range(QT):
                        last = nc.tensor.transpose(ps[:, 128 * i:128 * i + 128], x_tok[:, b, i, :], ident)
                    last.then_inc(j_full, 1)
                elif kind == "CQ":
                    b, = args
                    job_done(pe, "XT", 0, b)
                    for k, w in enumerate(("q", "qs")):
                        ps = bank(JOB[item] + k)
                        nc.tensor.matmul(ps[:, :], wx[:, W_X[w], :], xT[:, b, :], start=True, stop=True).then_inc(j_full, 1)
                elif kind == "LG":
                    b, = args
                    ps = bank(JOB[item])
                    job_done(pe, "XT", 1, b)
                    for i in range(QT):
                        last = nc.tensor.matmul(ps[:, E * i:E * i + E], xT[:, b, 128 * i:128 * i + 128], wg[:, :], start=True, stop=True)
                    last.then_inc(j_full, 1)
                elif kind == "WT":
                    b, = args
                    ps = bank(JOB[item])
                    pe.wait_ge(s_gw, b + 1)
                    for i in range(QT):
                        last = nc.tensor.transpose(ps[0:PARTS * E, 64 * i:64 * i + 64].bitcast(BF16),
                                                   gpart[:, i, :, :].rearrange("p a e -> p (a e)"), iden16)
                    last.then_inc(j_full, 1)
                elif kind == "BC":
                    b, e = args
                    ps = bank(JOB[item])
                    job_done(pe, "WT", b)
                    nc.tensor.matmul(ps[:, :], c16[0:PARTS * E, H_SEL + 128 * e:H_SEL + 128 * e + 128], gT[:, b, :],
                                     start=True, stop=True).then_inc(j_full, 1)
                elif kind == "F1":
                    b, f = args
                    if f == 0:
                        job_done(pe, "XT", 1, b)
                    pe.wait_ge(s_wl, WC)
                    three_products(ring_bank("A", item), wparts[0], b, f).then_inc(s_a, 1)
                elif kind == "F3":
                    b, f = args
                    pe.wait_ge(s_wl, 2 * WC)
                    three_products(ring_bank("B", item), wparts[1], b, f).then_inc(s_b, 1)
                elif kind == "F2":
                    b, f = args
                    n = FT * b + f
                    if f == 0:
                        pe.wait_ge(s_po, NU - NG - 1 if b == 0 else NU)
                        pe.wait_ge(s_w2, 16)
                    fill_done(pe, "B", [("F3", (b, f))])
                    nc.tensor.matmul(psO[b][:, :], w2[:, 128 * f:128 * f + 128], hid[:, n % 4, :], start=f == 0,
                                     stop=f == FT - 1).then_inc(s_y, 1)
                elif kind == "YT":
                    b, = args
                    ps = bank(JOB[item])
                    pe.wait_ge(s_yT, b + 1)
                    for i in range(QT):
                        last = nc.tensor.transpose(ps[:, 128 * i:128 * i + 128], yT[:, 128 * i:128 * i + 128], ident)
                    last.then_inc(j_full, 1)

        @block.scalar
        def _(act):
            def bank(n):
                act.wait_ge(j_full, n + 1)
                return psJ[n % 2]

            def free(n, ins):
                ins.then_inc(j_done[n % 2], 1)

            act.dma_start(wa[:, 0:3, :], wa_d[:, 0:3, :]).then_inc(s_first, 16)
            act.dma_start(c32[:, 0:2 * S], c32_d[:, 0:2 * S]).then_inc(s_turn, 16)
            act.dma_start(bcol[:, :], bcol_d).then_inc(s_iq, 16)
            act.dma_start(wa[:, 7:10, :], wa_d[:, 7:10, :]).then_inc(s_iv, 16)
            act.dma_start(c16[:, :], c16_d).then_inc(s_rest, 16)
            act.dma_start(ctxt[:, :, :], ctxt_d).then_inc(s_rest, 16)
            act.dma_start(wx[:, :, :], wx_d).then_inc(s_rest, 16)
            act.dma_start(wg[:, :], wg_d).then_inc(s_rest, 16)
            act.dma_start(c32[:, 2 * S:], c32_d[:, 2 * S:]).then_inc(s_rest, 16)

            for item in PLAN:
                kind, args = item
                if kind == "H":
                    b, w = args
                    n = 2 * b + (w == "k")
                    ps = bank(JOB[item])
                    if n == 0:
                        act.wait_ge(s_iq, 16 * 2)
                    if n >= 2:
                        act.wait_ge(s_sw[n - 2], 16 * PARTS)
                    nc.scalar.activation(part[:, n % 2, 0, :], ps[:, :], ACT.Identity, bias=bcol[:, n % 2:n % 2 + 1]).then_inc(s_p1, 1)
                elif kind == "H2":
                    b, w = args
                    n = 2 * b + (w == "k")
                    job_done(act, "H", b, w)
                    nc.scalar.activation(part[:, n % 2, 1, :], rest[:, n % 2, :], ACT.Copy).then_inc(s_p2, 1)
                elif kind == "CK":
                    act.wait_ge(s_cres, 1)
                    nc.scalar.activation(partc[:, 0, :, 0:SC], rest[:, 0, 0:B * SC].rearrange("p (b t) -> p b t", b=B),
                                         ACT.Copy).then_inc(s_cp1, 1)
                elif kind == "CK2":
                    act.wait_ge(s_cres, 2)
                    nc.scalar.activation(partc[:, 1, :, 0:SC], rest[:, 1, 0:B * SC].rearrange("p (b t) -> p b t", b=B),
                                         ACT.Copy).then_inc(s_cp2, 1)
                elif kind == "CQ":
                    b, = args
                    if b == 0:
                        act.wait_ge(s_sw[2], 16 * PARTS)
                        act.wait_ge(s_sw[3], 16 * PARTS)
                    act.wait_ge(s_cres, 2 * b + 3)
                    nc.scalar.activation(part[:, b, 0, :], rest[:, 0, :], ACT.Copy).then_inc(s_cp1, 1)
                elif kind == "CQ2":
                    b, = args
                    act.wait_ge(s_cres, 2 * b + 4)
                    nc.scalar.activation(part[:, b, 1, :], rest[:, 1, :], ACT.Copy).then_inc(s_cp2, 1)
                elif kind == "MT":
                    u, = args
                    st, b, g = unit(u)
                    ps = bank(JOB[item])
                    if u >= 2:
                        act.wait_ge(s_mr[u % 2], 16 * (u // 2))
                    free(JOB[item], nc.scalar.activation(mrow[:, u % 2, :], ps[0:PARTS * G, 0:256].bitcast(BF16), ACT.Copy))
                    job_done(act, "MT", u)
                    act.dma_start(qst[ROWS:ROWS + PARTS, b, G * g:G * g + G, :], mrow[:, u % 2, :]).then_inc(s_mr[u % 2], 16)
                elif kind == "B":
                    u, k = args
                    st, b, g = unit(u)
                    n = FILL["B"][item]
                    if k == 0 and u >= 2:
                        act.wait_ge(s_pv, u - 1)
                    act.wait_ge(s_b, n + 1)
                    ps = psB[n % 2]
                    if st == 0:
                        kt, j, _ = b_banks(u)[k][0]
                        if kt == 2:
                            half = (prob, prob_more)[j // 2]
                            dst = half[:, u % 2, :].rearrange("p (j c) -> p j c", j=2)[:, :, 1024:1280]
                            src = ps[:, :].rearrange("p (j c) -> p j c", j=2)
                        elif kt == 1:
                            half, c = (prob, prob_more)[j // 2], j % 2 * 1280
                            dst, src = half[:, u % 2, c + 512:c + 1024], ps[:, :]
                        else:
                            dst, src = prob_at(u, 0, j), ps[:, :]
                    else:
                        kt, j, _ = b_banks(u)[k][0]
                        dst, src = prob_at(u, kt, j), ps[:, :]
                    nc.scalar.activation(dst, src, ACT.Exp, scale=SCALE).then_inc(b_done[n % 2], 1)
                elif kind == "POC":
                    u, = args
                    act.wait_ge(s_pv, u + 1)
                    if u >= 2:
                        job_done(act, "OT", u - 2)
                    nc.scalar.activation(po_sb[:, u % 2, :], psO[po_bank(u)][:, :], ACT.Copy).then_inc(s_po, 1)
                elif kind == "ONT":
                    st, b = args
                    ps = bank(JOB[item])
                    if (st, b) != (0, 0):
                        job_done(act, "OP", *divmod(2 * st + b - 1, 2))
                    free(JOB[item], nc.scalar.activation(ot_sb[:, :], ps[:, :], ACT.Copy))
                elif kind == "XT":
                    st, b = args
                    ps = bank(JOB[item])
                    if st == 1:
                        nc.scalar.activation(xT[:, b, :], ps[:, :], ACT.Copy)
                        nc.scalar.activation(x_high[:, b, :], ps[:, :], ACT.Copy).then_inc(s_xh, 1)
                    else:
                        free(JOB[item], nc.scalar.activation(xT[:, b, :], ps[:, :], ACT.Copy))
                elif kind == "WS":
                    c, = args
                    cols = slice(c % WC * (FT * 128 // WC), (c % WC + 1) * (FT * 128 // WC))
                    act.wait_ge(s_wd[c % 2], 16 * (c // 2 + 1))
                    exps_done(act, NG * (c // WC + 1) - 1, range(len(b_banks(0))))
                    nc.scalar.activation(wparts[c // WC][0][:, cols], stage[:, c % 2, :], ACT.Copy).then_inc(s_wh, 1)
                elif kind == "BC":
                    b, e = args
                    n = E * b + e
                    if n == 0:
                        act.wait_ge(s_pv, B * NG)
                    if n >= 2:
                        act.wait_ge(s_sg, 2 * (n - 1))
                    ps = bank(JOB[item])
                    free(JOB[item], nc.scalar.activation(wbc[:, n % 2, :], ps[:, :], ACT.Copy, scale=0.5))
                elif kind == "WT":
                    b, = args
                    ps = bank(JOB[item])
                    if b == 0:
                        act.wait_ge(s_sw[5], 16 * (PARTS + 1))
                    free(JOB[item], nc.scalar.activation(gT[:, b, :], ps[0:PARTS * E, 0:256].bitcast(BF16), ACT.Copy))
                elif kind == "GATE":
                    b, = args
                    act.wait_ge(s_gd, b + 1)
                    nc.scalar.activation(gsm[:, 3, :], gsm[:, 2, :], ACT.Exp).then_inc(s_ge, 1)
                elif kind == "F1":
                    b, f = args
                    n = FT * b + f
                    a = FILL["A"][item]
                    act.wait_ge(s_a, a + 1)
                    if n >= 2:
                        act.wait_ge(s_sg, n - 1)
                    nc.scalar.activation(silu[:, n % 2, :], psA[a % 2][:, :], ACT.Tanh, scale=0.5).then_inc(s_th, 1)
                elif kind == "YE":
                    b, = args
                    act.wait_ge(s_y, FT * (b + 1))
                    if b == 1:
                        job_done(act, "YT", 0)
                    nc.scalar.activation(yT, psO[b][:, :], ACT.Copy).then_inc(s_yT, 1)

        @block.vector
        def _(dve):
            steps = [0]

            def link(ins):
                steps[0] += 1
                ins.then_inc(s_dve, 1)
                dve.wait_ge(s_dve, steps[0])

            def bank(n):
                dve.wait_ge(j_full, n + 1)
                return psJ[n % 2]

            def free(n, ins):
                ins.then_inc(j_done[n % 2], 1)

            for item in PLAN:
                kind, args = item
                if kind == "U":
                    b, w = args
                    n = 3 * b + "qkv".index(w)
                    if n == 0:
                        dve.wait_ge(s_turn, 16)
                    ps = bank(JOB[item])
                    if n >= 2:
                        before = [i for i in PLAN if i[0] in ("H", "VH")][n - 2]
                        dve.wait_ge(j_full, JOB[before] + 1)
                    nc.vector.tensor_tensor(ab[:, n % 2, 0, :], ps[:, :], c32[:, C_CA:C_CA + S], ALU.mult)
                    free(JOB[item], nc.vector.tensor_tensor(ab[:, n % 2, 1, :], ps[:, :], c32[:, C_SA:C_SA + S], ALU.mult))
                elif kind == "H":
                    b, w = args
                    n = 2 * b + (w == "k")
                    ps = bank(JOB[item])
                    dve.wait_ge(s_p1, n + 1)
                    nc.vector.scalar_tensor_tensor(out=rest[:, n % 2, :], in0=ps[:, :], scalar=bcol[:, n % 2:n % 2 + 1],
                                                   in1=part[:, n % 2, 0, :], op0=ALU.add, op1=ALU.subtract).then_inc(j_done[JOB[item] % 2], 1)
                elif kind == "H2":
                    b, w = args
                    n = 2 * b + (w == "k")
                    dve.wait_ge(s_p2, n + 1)
                    nc.vector.tensor_tensor(part[:, n % 2, 2, :], rest[:, n % 2, :], part[:, n % 2, 1, :], ALU.subtract).then_inc(s_p3, 1)
                elif kind == "VH":
                    b, = args
                    ps = bank(JOB[item])
                    dve.wait_ge(s_zero, b + 1)
                    dve.wait_ge(s_row, 16)
                    tiles = lambda x: x.rearrange("p (i h d) -> p i h d", i=QT, h=H)
                    bias = brow[:, 0, :].rearrange("p (h d) -> p h d", h=H).unsqueeze(1).to_broadcast([128, QT, H, HD])
                    free(JOB[item], nc.vector.tensor_tensor(v_sb[b][:, :, :, 0:HD], tiles(ps[:, :]), bias, ALU.add))
                elif kind == "CK":
                    n = JOB[item]
                    tw = lambda x: x.rearrange("p (b t) -> p b t", b=B)
                    for k, c in enumerate((C_CK, C_SK)):
                        ps = bank(n + k)
                        if k == 0:
                            dve.wait_ge(s_p2, 2 * B)
                            dve.wait_ge(s_p3, 2 * B)
                        ins = nc.vector.scalar_tensor_tensor(out=tw(rest[:, k, 0:B * SC]), in0=tw(ps[:, 0:B * SC]), scalar=bcol[:, 4 + k:5 + k],
                                                             in1=c32[:, c:c + SC].unsqueeze(1).to_broadcast([128, B, SC]), op0=ALU.add, op1=ALU.mult)
                        free(n + k, ins)
                    dve.wait_ge(j_done[n % 2], n // 2 + 1)
                    dve.wait_ge(j_done[(n + 1) % 2], (n + 1) // 2 + 1)
                    nc.vector.tensor_tensor(rest[:, 0, 0:B * SC], rest[:, 0, 0:B * SC], rest[:, 1, 0:B * SC], ALU.add).then_inc(s_cres, 1)
                elif kind == "CK2":
                    tw = lambda x: x.rearrange("p (b t) -> p b t", b=B)
                    dve.wait_ge(s_cres, 1)
                    dve.wait_ge(s_cp1, 1)
                    dve.wait_ge(s_zero, 1)
                    nc.vector.tensor_tensor(tw(rest[:, 1, 0:B * SC]), tw(rest[:, 0, 0:B * SC]), partc[:, 0, :, 0:SC], ALU.subtract).then_inc(s_cres, 1)
                elif kind == "CK3":
                    tw = lambda x: x.rearrange("p (b t) -> p b t", b=B)
                    dve.wait_ge(s_cres, 2)
                    dve.wait_ge(s_cp2, 1)
                    nc.vector.tensor_tensor(partc[:, 2, :, 0:SC], tw(rest[:, 1, 0:B * SC]), partc[:, 1, :, 0:SC], ALU.subtract).then_inc(s_cp3, 1)
                elif kind == "CV":
                    ps = bank(JOB[item])
                    dve.wait_ge(s_zero, 3 + G)
                    heads = lambda x: x.rearrange("p (h d) -> p h d", h=H)
                    for b in range(B):
                        nc.vector.tensor_tensor(vc_sb[:, b, :, 0:HD], heads(ps[:, 128 * b:128 * b + 128]), heads(brow[:, 2, :]), ALU.add)
                    for b in range(B):
                        for j in range(G):
                            rows = slice(32 * j, 32 * j + TAIL)
                            pick = lambda x: x.rearrange("p (g j d) -> p g j d", g=NG, j=G)[:, :, j, :]
                            last = nc.vector.tensor_tensor(vblk[rows, b, :, j, 0:HD], pick(ps[rows, 128 * (B + b):128 * (B + b) + 128]),
                                                           pick(brow[rows, 2, :]), ALU.add)
                    free(JOB[item], last)
                elif kind == "A":
                    u, k = args
                    n = FILL["A"][item]
                    blocks, width = a_banks(u)[k]
                    dve.wait_ge(s_a, n + 1)
                    if k == 0 and u >= 2:
                        dve.wait_ge(s_mp, u - 1)
                    nb = len(blocks)
                    c = blocks[0][0] * G + blocks[0][1]
                    nc.vector.tensor_reduce(negm[:, u % 2, :, :].rearrange("p i j -> p (i j)")[:, c:c + nb],
                                            psA[n % 2][:, 0:nb * width].rearrange("p (m w) -> p m w", m=nb), AX.X, ALU.max,
                                            negate=True).then_inc(a_done[n % 2], 1)
                elif kind == "OT":
                    u, = args
                    st, b, g = unit(u)
                    ps = bank(JOB[item])
                    if g == 0 and u > 0:
                        job_done(dve, "ONT", *divmod(u // NG - 1, 2))
                    o = ps[:, :].rearrange("p (i j c) -> p i j c", i=QT, j=G)
                    link(nc.vector.reciprocal(rec[:, u % 2, :, :], o[:, :, :, HD]))
                    ins = nc.vector.tensor_tensor(onorm[:, :, 32 * g:32 * g + 32].rearrange("p i (j d) -> p i j d", j=G), o[:, :, :, 0:HD],
                                                  rec[:, u % 2, :, :].unsqueeze(3).to_broadcast([128, QT, G, HD]), ALU.mult)
                    free(JOB[item], ins)
                elif kind in ("OP", "YT"):
                    st, b = args if kind == "OP" else (2, args[0])
                    ps = bank(JOB[item])
                    if st == 0:
                        dve.wait_ge(s_xb, 1)
                    res = x_tok[:, b, :, :]
                    ins = nc.vector.tensor_tensor(z[:, :, :], ps[:, :].rearrange("p (i d) -> p i d", i=QT), res, ALU.add)
                    free(JOB[item], ins)
                    dve.wait_ge(j_done[JOB[item] % 2], JOB[item] // 2 + 1)
                    if st == 1:
                        link(nc.vector.tensor_tensor(z[:, :, :], z[:, :, :], brow[:, 3:4, :].to_broadcast([128, QT, D]), ALU.add))
                elif kind == "LN":
                    st, b = args
                    n = 2 * st + b
                    for i in range(QT):
                        last = nc.vector.bn_stats(stats[:, i, :], z[:, i, :])
                    link(last)
                    for i in range(QT):
                        last = nc.vector.bn_aggr(mv[:, i, :], stats[:, i, :])
                    last.then_inc(s_mv, 1)
                elif kind == "LNX":
                    st, b = args
                    n = 2 * st + b
                    dve.wait_ge(s_rs, n + 1)
                    for i in range(QT):
                        last = nc.vector.tensor_scalar(x_tok[:, b, i, :], z[:, i, :], mv[:, i, 0:1], rstd[:, i:i + 1], ALU.subtract, ALU.mult)
                    last.then_inc(s_x, 1)
                elif kind == "CQ":
                    b, = args
                    n = JOB[item]
                    for k, c in enumerate((C_CQ, C_SQ)):
                        ps = bank(n + k)
                        if k == 0:
                            dve.wait_ge(s_cp2, b + 1)
                        ins = nc.vector.scalar_tensor_tensor(out=rest[:, k, :], in0=ps[:, :], scalar=bcol[:, 2 + k:3 + k],
                                                             in1=c32[:, c:c + S], op0=ALU.add, op1=ALU.mult)
                        free(n + k, ins)
                    dve.wait_ge(j_done[n % 2], n // 2 + 1)
                    dve.wait_ge(j_done[(n + 1) % 2], (n + 1) // 2 + 1)
                    nc.vector.tensor_tensor(rest[:, 0, :], rest[:, 0, :], rest[:, 1, :], ALU.add).then_inc(s_cres, 1)
                elif kind == "CQ2":
                    b, = args
                    dve.wait_ge(s_cres, 2 * b + 3)
                    dve.wait_ge(s_cp1, b + 2)
                    nc.vector.tensor_tensor(rest[:, 1, :], rest[:, 0, :], part[:, b, 0, :], ALU.subtract).then_inc(s_cres, 1)
                elif kind == "CQ3":
                    b, = args
                    dve.wait_ge(s_cres, 2 * b + 4)
                    dve.wait_ge(s_cp2, b + 2)
                    nc.vector.tensor_tensor(part[:, b, 2, :], rest[:, 1, :], part[:, b, 1, :], ALU.subtract).then_inc(s_cp3, 1)
                elif kind == "GATE":
                    b, = args
                    job = JOB[("LG", (b,))]
                    ps = bank(job)
                    lg = ps[:, 0:QT * E].rearrange("p (i e) -> p i e", i=QT)
                    for i in range(QT):
                        last = nc.vector.max(top[:, i, :], lg[:, i, :])
                    link(last)
                    for i in range(QT):
                        last = nc.vector.max_index(tix[:, i, :], top[:, i, :], lg[:, i, :])
                    free(job, last)
                    dve.wait_ge(j_done[job % 2], job // 2 + 1)
                    first, second = gsm[:, 0, :], gsm[:, 1, :]
                    link(nc.vector.tensor_copy(first, tix[:, :, 0]))
                    link(nc.vector.tensor_copy(second, tix[:, :, 1]))
                    nc.vector.tensor_tensor(gsm[:, 2, :], top[:, :, 1], top[:, :, 0], ALU.subtract).then_inc(s_gd, 1)
                elif kind == "GATE2":
                    b, = args
                    dve.wait_ge(s_ge, b + 1)
                    link(nc.vector.tensor_scalar(gsm[:, 4, :], gsm[:, 3, :], 1.0, None, ALU.add))
                    link(nc.vector.reciprocal(gsm[:, 4, :], gsm[:, 4, :]))
                    link(nc.vector.tensor_tensor(gsm[:, 5, :], gsm[:, 3, :], gsm[:, 4, :], ALU.mult))
                elif kind == "GATE3":
                    b, = args
                    first, second = gsm[:, 0, :], gsm[:, 1, :]
                    full = lambda x: x.unsqueeze(2).to_broadcast([128, QT, E])
                    iota = c32[:, C_IOTA:C_IOTA + E].unsqueeze(1).to_broadcast([128, QT, E])
                    link(nc.vector.tensor_tensor(gw[:, 0, :, :], iota, full(first), ALU.is_equal))
                    link(nc.vector.tensor_tensor(gw[:, 0, :, :], gw[:, 0, :, :], full(gsm[:, 4, :]), ALU.mult))
                    link(nc.vector.tensor_tensor(gw[:, 1, :, :], iota, full(second), ALU.is_equal))
                    link(nc.vector.tensor_tensor(gw[:, 1, :, :], gw[:, 1, :, :], full(gsm[:, 5, :]), ALU.mult))
                    link(nc.vector.tensor_tensor(gw[:, 0, :, :], gw[:, 0, :, :], gw[:, 1, :, :], ALU.add))
                    if b > 0:
                        job_done(dve, "WT", b - 1)
                    link(nc.vector.tensor_copy(gpart[:, :, 0, :], gw[:, 0, :, :]))
                    link(nc.vector.tensor_tensor(gw[:, 2, :, :], gw[:, 0, :, :], gpart[:, :, 0, :], ALU.subtract))
                    link(nc.vector.tensor_copy(gpart[:, :, 1, :], gw[:, 2, :, :]))
                    nc.vector.tensor_tensor(gpart[:, :, 2, :], gw[:, 2, :, :], gpart[:, :, 1, :], ALU.subtract).then_inc(s_gw, 1)
                elif kind == "XT" and args[0] == 1:
                    _, b = args
                    dve.wait_ge(s_xh, b + 1)
                    ps = bank(JOB[item])
                    free(JOB[item], nc.vector.tensor_tensor(x_low[:, b, :], ps[:, :], x_high[:, b, :].bitcast(FP32), ALU.subtract))
                elif kind == "F1":
                    b, f = args
                    n = FT * b + f
                    a = FILL["A"][item]
                    dve.wait_ge(s_th, n + 1)
                    nc.vector.scalar_tensor_tensor(out=silu[:, n % 2, :], in0=silu[:, n % 2, :], scalar=1.0, in1=psA[a % 2][:, :],
                                                   op0=ALU.add, op1=ALU.mult).then_inc(a_done[a % 2], 1)
                elif kind == "F3":
                    b, f = args
                    n = FT * b + f
                    h = FILL["B"][item]
                    dve.wait_ge(s_b, h + 1)
                    dve.wait_ge(s_sg, n + 1)
                    if n >= 4:
                        dve.wait_ge(s_y, n - 3)
                    nc.vector.tensor_tensor(hid[:, n % 4, :], psB[h % 2][:, :], gated[:, n % 2, :], ALU.mult).then_inc(b_done[h % 2], 1)


_ATTN_Q = [8 * (4 * (p // 32) + p % 4) + p % 32 // 4 for p in range(128)]


def constants():
    f = np.float32
    i = np.arange(D // 2, dtype=f)
    theta = (10000.0 ** (-2.0 * (i.astype(np.float64) - 1.0) / D)).astype(f)
    ang = np.arange(S, dtype=f)[:, None] * theta[None, :]
    c, s = np.cos(ang).astype(f), np.sin(ang).astype(f)
    c32 = np.zeros((128, NC32), f)
    c32[:, C_CA:C_CA + S] = np.repeat(c, 2, axis=1).T
    sa = np.repeat(s, 2, axis=1).T.copy()
    sa[0::2] *= -1
    c32[:, C_SA:C_SA + S] = sa

    inv = (1.0 / 10000.0 ** (np.arange(0, HD, 2, dtype=np.float64) / HD)).astype(f)
    dim = np.arange(128) % 32 // 4
    sign = np.where(dim < HD // 2, -1, 1).astype(f)[:, None]
    for n, cc, cs in ((S, C_CQ, C_SQ), (SC, C_CK, C_SK)):
        t = np.arange(n, dtype=f)
        fr = np.outer(f(10.0) * (t / f(n)), inv).astype(f)
        c32[:, cc:cc + n] = np.cos(fr).astype(f).T[dim % (HD // 2)]
        c32[:, cs:cs + n] = np.sin(fr).astype(f).T[dim % (HD // 2)] * sign
    c32[:, C_ID:C_ID + 128] = np.eye(128)
    c32[:, C_IOTA:C_IOTA + E] = np.arange(E)
    c32[:, C_POW:C_POW + QT] = -0.5
    bf = np.dtype("bfloat16")
    c16 = np.zeros((128, NC16), f)
    c16[:, H_ID:H_ID + 128] = np.eye(128)
    q, k = np.arange(128)[:, None], np.arange(128)[None, :]
    c16[:, H_MA:H_MA + 128] = np.where(k > q, NEG, 0)
    c16[:, H_MB:H_MB + 128] = np.where(q > k, NEG, 0)
    for e in range(E):
        for a in range(PARTS):
            c16[E * a + e, H_SEL + 128 * e:H_SEL + 128 * e + 128] = 1
    tail = np.zeros((KR - ROWS, 2, S), f)
    tail[:PARTS, 1] = 1
    tailc = np.zeros((KR - ROWS, SCP), f)
    tailc[:PARTS, :SC] = 1
    return c32, c16.astype(bf), np.concatenate([tail.ravel(), tailc.ravel()]).astype(bf)


def kernel(**inputs):
    import concourse.bacc as bacc
    from concourse.bass_utils import run_bass_kernel_spmd as run

    a = {k: np.asarray(v) for k, v in inputs.items()}
    order, swap2, swap4 = np.array(_ATTN_Q), np.arange(D) ^ 1, np.arange(D) ^ 4
    ip, ib = a["L0_attn_in_proj_w"], a["L0_attn_in_proj_b"]
    iq, ik, iv = ip[0:D], ip[D:2 * D], ip[2 * D:3 * D]
    wa = [a["L0_attn_wq"].T, a["L0_attn_wk"].T, a["L0_attn_wv"].T,
          iq[order].T, iq[order].T[swap2], ik[order].T, ik[order].T[swap2], iv.T, iv.T[swap2], a["L0_attn_out_w"].T]
    xq, xk = a["L0_xattn_Wq"], a["L0_xattn_Wk"]
    wx = [xq[order].T, xq[swap4][order].T, xk[order].T, xk[swap4][order].T, a["L0_xattn_Wv"].T, a["L0_xattn_Wo"].T]
    bq, bk = a["L0_xattn_bq"], a["L0_xattn_bk"]
    bcol = [ib[0:D][order], ib[D:2 * D][order], bq[order], bq[swap4][order], bk[order], bk[swap4][order]]
    brow = [ib[2 * D:], a["L0_attn_out_b"], a["L0_xattn_bv"], a["L0_xattn_bo"]]
    c32, c16, tail = constants()
    arrays = {
        "xt": a["x"].transpose(2, 0, 1), "x": a["x"], "ctxt": a["ctx_1024"].transpose(2, 0, 1),
        "wa": np.stack(wa, axis=1), "wx": np.stack(wx, axis=1), "wg": a["L0_ffn_wg"].T,
        "bcol": np.stack(bcol, axis=1), "brow": np.concatenate(brow),
        "c32": c32, "c16": c16, "tail": tail,
        "w1": a["L0_ffn_w1"].reshape(E * I, D).T, "w3": a["L0_ffn_w3"].reshape(E * I, D).T,
        "w2": a["L0_ffn_w2"].transpose(0, 2, 1).reshape(FT, 128, D).transpose(1, 0, 2).reshape(128, FT * D),
    }
    arrays = {k: np.ascontiguousarray(v) for k, v in arrays.items()}
    nc = bacc.Bacc("TRN2", target_bir_lowering=False, num_devices=1)
    args = [nc.dram_tensor(k + "_dram", v.shape, mybir.dt.from_np(v.dtype), kind="ExternalInput").ap() for k, v in arrays.items()]
    out = nc.dram_tensor("out_dram", (B, S, D), FP32, kind="ExternalOutput").ap()
    layer_kernel(nc, *args, out)
    r = run(nc, [{k + "_dram": v for k, v in arrays.items()}], core_ids=[0])
    return r.results[0]["out_dram"]
```
